# Optimizing a Trainium2 kernel written in Bass

```python
import numpy as np
import jax
import jax.numpy as jnp

def _softmax(x, axis=-1):
    return jax.nn.softmax(x, axis=axis)

def _gelu(x):
    return jax.nn.gelu(x, approximate=True)

def _silu(x):
    return jax.nn.silu(x)

def _sigmoid(x):
    return jax.nn.sigmoid(x)

def _layernorm(x, axis=-1, eps=1e-05):
    m = jnp.mean(x, axis=axis, keepdims=True)
    v = jnp.var(x, axis=axis, keepdims=True)
    return (x - m) / jnp.sqrt(v + eps)

def _scatter_add(tgt, idx, src, axis=0):
    return tgt.at[idx].add(src)

def _segment_sum(src, seg, n):
    return jax.ops.segment_sum(src, seg, n)
kernel_name = 'mk_perceiver_d1_seqx_r8_b17c1d'

def setup_inputs(seed: int=0):
    np.random.seed(seed)
    _w = jnp.asarray

    def _rec_inputs():
        import jax
        import jax.numpy as jnp
        _rk = jax.random.key(seed)
        x = 7.22e-05 + 1 * jax.random.normal(jax.random.fold_in(_rk, 1), (2, 128, 128), jnp.float32)
        _lenS = 128 - jax.random.randint(jax.random.fold_in(_rk, 7), (2,), 0, max(1, 128 // 4) + 1, jnp.int32)
        _lenS2 = 2048 - jax.random.randint(jax.random.fold_in(_rk, 8), (2,), 0, max(1, 2048 // 4) + 1, jnp.int32)
        _ctx_1024P = jax.random.normal(jax.random.fold_in(_rk, 11), (2, 16, 128), jnp.float32)
        _ctx_1024c = jax.random.dirichlet(jax.random.fold_in(_rk, 511), 0.3 * jnp.ones((16,), jnp.float32), (2, 2048))
        _ctx_1024t = jnp.einsum('bsk,bkd->bsd', _ctx_1024c, _ctx_1024P)
        _ctx_1024t = _ctx_1024t * jax.lax.rsqrt(jnp.mean(jnp.square(_ctx_1024t)) + 1e-12) * 0.953939
        ctx_1024 = 4.13588e-05 + 0.999923 * (_ctx_1024t + 0.3 * jax.random.normal(jax.random.fold_in(_rk, 611), (2, 2048, 128), jnp.float32))
        return (x, ctx_1024)
    x, ctx_1024 = _rec_inputs()

    def _L0_xattn_setup():
        import jax, jax.numpy as jnp
        import numpy as np
        D_MODEL = 128
        NUM_HEADS = 16
        D_K = D_MODEL // NUM_HEADS
        CLAMP = 1000000000.0
        EPS = 1e-12

        def _split_heads(x):
            b, s, _ = x.shape
            return x.reshape(b, s, NUM_HEADS, D_K).transpose(0, 2, 1, 3)
        key = jax.random.key(seed)
        ks = jax.random.split(key, 11)
        B, S, D = (4, 256, D_MODEL)
        std = 1.0 / np.sqrt(D)
        inp = {'Q': jax.random.normal(ks[0], (B, S, D), jnp.float32), 'K': jax.random.normal(ks[1], (B, S, D), jnp.float32), 'V': jax.random.normal(ks[2], (B, S, D), jnp.float32), 'Wq': jax.random.normal(ks[3], (D, D), jnp.float32) * std, 'bq': jnp.zeros((D,), jnp.float32), 'Wk': jax.random.normal(ks[4], (D, D), jnp.float32) * std, 'bk': jnp.zeros((D,), jnp.float32), 'Wv': jax.random.normal(ks[5], (D, D), jnp.float32) * std, 'bv': jnp.zeros((D,), jnp.float32), 'Wo': jax.random.normal(ks[6], (D, D), jnp.float32) * std, 'bo': jnp.zeros((D,), jnp.float32)}
        return inp
    _L0_xattn_all = _L0_xattn_setup()
    _L0_xattn_in = {k: v for k, v in _L0_xattn_all.items() if k in ('Wq', 'bq', 'Wk', 'bk', 'Wv', 'bv', 'Wo', 'bo')}
    del _L0_xattn_all

    def _L0_attn_setup():
        import jax, jax.numpy as jnp
        import numpy as np
        import math
        DIM = 128
        NUM_HEADS = 16
        HEAD_DIM = DIM // NUM_HEADS
        MAX_BIAS = 8.0
        SCALE = HEAD_DIM ** (-0.5)

        def _alibi_slopes(n):

            def pow2(n):
                start = 2.0 ** (-2.0 ** (-(math.log2(n) - 3)))
                return [start * start ** i for i in range(n)]
            if math.log2(n).is_integer():
                return pow2(n)
            c = 2 ** math.floor(math.log2(n))
            return pow2(c) + _alibi_slopes(2 * c)[0::2][:n - c]

        def _rotate_half(t):
            t1, t2 = jnp.split(t, 2, axis=-1)
            return jnp.concatenate([-t2, t1], axis=-1)
        key = jax.random.key(seed)
        k1, k2, k3, k4 = jax.random.split(key, 4)
        B, N, C = (2, 256, DIM)
        x = jax.random.normal(k1, (B, N, C), dtype=jnp.float32)
        qkv_w = jax.random.normal(k2, (3 * C, C), dtype=jnp.float32) * C ** (-0.5)
        proj_w = jax.random.normal(k3, (C, C), dtype=jnp.float32) * C ** (-0.5)
        proj_b = jax.random.normal(k4, (C,), dtype=jnp.float32) * 0.01
        slopes = jnp.asarray(np.array(_alibi_slopes(NUM_HEADS), dtype=np.float32))
        return {'x': x, 'qkv_w': qkv_w, 'proj_w': proj_w, 'proj_b': proj_b, 'slopes': slopes}
    _L0_attn_all = _L0_attn_setup()
    _L0_attn_in = {k: v for k, v in _L0_attn_all.items() if k in ('qkv_w', 'proj_w', 'proj_b', 'slopes')}
    del _L0_attn_all

    def _L0_ffn_setup():
        import jax, jax.numpy as jnp
        import numpy as np
        B, L, D = (4, 64, 128)
        E, TOP_K = (16, 4)
        F = 4 * D
        key = jax.random.key(seed)
        ks = jax.random.split(key, 6)
        scale = 0.02
        return {'x': jax.random.normal(ks[0], (B, L, D), jnp.float32), 'keys': jax.random.normal(ks[1], (E, D), jnp.float32), 'w1': jax.random.normal(ks[2], (E, F, D), jnp.float32) * scale, 'b1': jnp.zeros((E, F), jnp.float32), 'w2': jax.random.normal(ks[3], (E, D, F), jnp.float32) * scale, 'b2': jnp.zeros((E, D), jnp.float32), 'rw': jax.random.normal(ks[4], (E, D), jnp.float32) * scale, 'rb': jnp.zeros((E,), jnp.float32)}
    _L0_ffn_all = _L0_ffn_setup()
    _L0_ffn_in = {k: v for k, v in _L0_ffn_all.items() if k in ('keys', 'w1', 'b1', 'w2', 'b2', 'rw', 'rb')}
    del _L0_ffn_all
    return {'x': x, 'ctx_1024': ctx_1024, 'L0_xattn_Wq': _L0_xattn_in['Wq'], 'L0_xattn_bq': _L0_xattn_in['bq'], 'L0_xattn_Wk': _L0_xattn_in['Wk'], 'L0_xattn_bk': _L0_xattn_in['bk'], 'L0_xattn_Wv': _L0_xattn_in['Wv'], 'L0_xattn_bv': _L0_xattn_in['bv'], 'L0_xattn_Wo': _L0_xattn_in['Wo'], 'L0_xattn_bo': _L0_xattn_in['bo'], 'L0_attn_qkv_w': _L0_attn_in['qkv_w'], 'L0_attn_proj_w': _L0_attn_in['proj_w'], 'L0_attn_proj_b': _L0_attn_in['proj_b'], 'L0_attn_slopes': _L0_attn_in['slopes'], 'L0_ffn_keys': _L0_ffn_in['keys'], 'L0_ffn_w1': _L0_ffn_in['w1'], 'L0_ffn_b1': _L0_ffn_in['b1'], 'L0_ffn_w2': _L0_ffn_in['w2'], 'L0_ffn_b2': _L0_ffn_in['b2'], 'L0_ffn_rw': _L0_ffn_in['rw'], 'L0_ffn_rb': _L0_ffn_in['rb']}

def reference(x, ctx_1024, L0_xattn_Wq, L0_xattn_bq, L0_xattn_Wk, L0_xattn_bk, L0_xattn_Wv, L0_xattn_bv, L0_xattn_Wo, L0_xattn_bo, L0_attn_qkv_w, L0_attn_proj_w, L0_attn_proj_b, L0_attn_slopes, L0_ffn_keys, L0_ffn_w1, L0_ffn_b1, L0_ffn_w2, L0_ffn_b2, L0_ffn_rw, L0_ffn_rb):
    import jax
    import jax.numpy as jnp

    def _L0_xattn_ref(Q, K, V, Wq, bq, Wk, bk, Wv, bv, Wo, bo):
        import jax, jax.numpy as jnp
        import numpy as np
        D_MODEL = 128
        NUM_HEADS = 16
        D_K = D_MODEL // NUM_HEADS
        CLAMP = 1000000000.0
        EPS = 1e-12

        def _split_heads(x):
            b, s, _ = x.shape
            return x.reshape(b, s, NUM_HEADS, D_K).transpose(0, 2, 1, 3)
        Qh = _split_heads(Q @ Wq.T + bq)
        Kh = _split_heads(K @ Wk.T + bk)
        Vh = _split_heads(V @ Wv.T + bv)
        scale = jnp.sqrt(jnp.asarray(D_K, Qh.dtype))
        scores = jnp.einsum('bhqd,bhkd->bhqk', Qh, Kh) / scale
        scores = scores - jnp.max(scores, axis=-1, keepdims=True)
        scores = jnp.clip(scores, -CLAMP, CLAMP)
        attn = jax.nn.softmax(scores, axis=-1)
        attn = jnp.clip(attn, EPS, None)
        attn = attn / jnp.sum(attn, axis=-1, keepdims=True)
        ctx = jnp.einsum('bhqk,bhkd->bhqd', attn, Vh)
        b, h, s, dk = ctx.shape
        ctx = ctx.transpose(0, 2, 1, 3).reshape(b, s, D_MODEL)
        return ctx @ Wo.T + bo

    def _L0_attn_ref(x, qkv_w, proj_w, proj_b, slopes):
        import jax, jax.numpy as jnp
        import numpy as np
        import math
        DIM = 128
        NUM_HEADS = 16
        HEAD_DIM = DIM // NUM_HEADS
        MAX_BIAS = 8.0
        SCALE = HEAD_DIM ** (-0.5)

        def _alibi_slopes(n):

            def pow2(n):
                start = 2.0 ** (-2.0 ** (-(math.log2(n) - 3)))
                return [start * start ** i for i in range(n)]
            if math.log2(n).is_integer():
                return pow2(n)
            c = 2 ** math.floor(math.log2(n))
            return pow2(c) + _alibi_slopes(2 * c)[0::2][:n - c]

        def _rotate_half(t):
            t1, t2 = jnp.split(t, 2, axis=-1)
            return jnp.concatenate([-t2, t1], axis=-1)
        B, N, C = x.shape
        H, D = (NUM_HEADS, HEAD_DIM)
        qkv = (x @ qkv_w.T).reshape(B, N, 3, H, D).transpose(2, 0, 3, 1, 4)
        q, k, v = (qkv[0], qkv[1], qkv[2])
        inv_freq = 1.0 / 10000.0 ** (jnp.arange(0, D, 2, dtype=jnp.float32) / D)
        freqs = jnp.arange(N, dtype=jnp.float32)[:, None] * inv_freq[None, :]
        sin = jnp.tile(jnp.sin(freqs), (1, 2))
        cos = jnp.tile(jnp.cos(freqs), (1, 2))
        q = q * cos + _rotate_half(q) * sin
        k = k * cos + _rotate_half(k) * sin
        attn = jnp.einsum('bhqd,bhkd->bhqk', q, k) * SCALE
        pos = jnp.arange(N, dtype=jnp.float32)
        diff = pos[None, :] - pos[:, None]
        diff = jnp.where(diff > 0, 0.0, diff)
        alibi = diff[None, :, :] * slopes[:, None, None] * MAX_BIAS
        attn = attn + alibi[None]
        w = jax.nn.softmax(attn, axis=-1)
        out = jnp.einsum('bhqk,bhkd->bhqd', w, v)
        out = out.transpose(0, 2, 1, 3).reshape(B, N, C)
        return out @ proj_w.T + proj_b

    def _L0_ffn_ref(x, keys, w1, b1, w2, b2, rw, rb):
        import jax, jax.numpy as jnp
        import numpy as np
        B, L, D = (4, 64, 128)
        E, TOP_K = (16, 4)
        F = 4 * D
        diff = x[:, :, None, :] - keys
        dist2 = jnp.sum(diff * diff, axis=-1)
        logits = -dist2 + jnp.einsum('bld,ed->ble', x, rw) + rb
        topv, topi = jax.lax.top_k(logits, TOP_K)
        w = jax.nn.softmax(topv, axis=-1)
        hidden = jax.nn.gelu(jnp.einsum('bld,efd->blef', x, w1) + b1, approximate=False)
        exp_out = jnp.einsum('blef,edf->bled', hidden, w2) + b2
        sel = jnp.take_along_axis(exp_out, topi[..., None], axis=2)
        fused = jnp.sum(w[..., None] * sel, axis=2)
        return fused
    x = x + _L0_xattn_ref(_layernorm(x, axis=-1), ctx_1024, ctx_1024, L0_xattn_Wq, L0_xattn_bq, L0_xattn_Wk, L0_xattn_bk, L0_xattn_Wv, L0_xattn_bv, L0_xattn_Wo, L0_xattn_bo)
    x = x + _L0_attn_ref(_layernorm(x, axis=-1), L0_attn_qkv_w, L0_attn_proj_w, L0_attn_proj_b, L0_attn_slopes)
    x = x + _L0_ffn_ref(_layernorm(x, axis=-1), L0_ffn_keys, L0_ffn_w1, L0_ffn_b1, L0_ffn_w2, L0_ffn_b2, L0_ffn_rw, L0_ffn_rb)
    return x

_drawn_inputs = setup_inputs


def setup_inputs(seed=0):
    import zlib

    import numpy as np

    out = dict(_drawn_inputs(seed))
    spreads = {'L0_xattn_bq': (0.0, 0.294),
     'L0_xattn_bk': (0.0, 2.0),
     'L0_xattn_bv': (0.0, 0.1),
     'L0_xattn_bo': (0.0, 0.1),
     'L0_ffn_b1': (0.0, 0.43),
     'L0_ffn_b2': (0.0, 0.1),
     'L0_ffn_rb': (0.0, 2.0)}
    factors = {'L0_attn_proj_b': 6.533, 'L0_ffn_rw': 8.0}
    for name, (base, spread) in spreads.items():
        noise = np.random.default_rng([zlib.crc32(name.encode()), seed]).standard_normal(out[name].shape)
        drawn = base * np.exp(spread * noise) if base else spread * noise
        out[name] = jnp.asarray(drawn.astype(out[name].dtype))
    for name, factor in factors.items():
        out[name] = (out[name] * factor).astype(out[name].dtype)
    return out
```

```python
import math

import numpy as np

import concourse.bass as bass
from concourse import mybir
from contextlib import ExitStack

B, S, D, H = 2, 128, 128, 16
DK = D // H
CTX = 2048
E, F, TOP = 16, 512, 4
FC = F // 128
NK = CTX // 128
PAIRS = H // 2
GH = 4
NG = H // GH
HALF = 64
M_ROWS = 3
TERM0 = 8
TERMS = [(0, 0), (0, 1), (1, 0), (1, 1), (0, 2), (2, 0), (1, 2)]
SCALE = DK ** -0.5
LN_EPS = 1e-5
CLIP = 1e-12
MAX_BIAS = 8.0
ONES2 = 0x3F803F80


def build(nc, x, ctxT, wq, wk, wv, wo, bq, bk, bv, bo, qkvw, projw, projb, slopes,
          keysT, w1, b1, w2, b2, rwT, rb, ident_in, blocks_in, rot_in, dist_in, tri_in, quart_in, sumrow_in, ones_in, out):
    fp32, bf16, i32 = mybir.dt.float32, mybir.dt.bfloat16, mybir.dt.int32
    ALU, ACT, AX = mybir.AluOpType, mybir.ActivationFunctionType, mybir.AxisListType

    with ExitStack() as es:
        def sb(name, shape, dt=fp32):
            return es.enter_context(nc.sbuf_tensor(name, shape, dt))

        def sem(name):
            return es.enter_context(nc.semaphore(name))

        ident = sb("ident", [128, 128])
        identb = sb("identb", [128, 128], bf16)
        blocks = sb("blocks", [128, H])
        blocksb = sb("blocksb", [128, H], bf16)
        rot = sb("rot", [128, 2, DK])
        dist = sb("dist", [128, 128])
        tri = sb("tri", [128, E, E])
        quart = sb("quart", [128, GH])
        sumrow = sb("sumrow", [128, GH])
        xs = sb("xs", [128, B, D])
        cT = sb("cT", [128, B, CTX])
        wqs, wks, wvs, wos = (sb(n, [128, 128]) for n in ("wqs", "wks", "wvs", "wos"))
        qkvs = sb("qkvs", [128, 3 * D])
        projs = sb("projs", [128, D])
        cols = sb("cols", [128, 4])
        bvB, boB, pbB, slB = (sb(n, [128, w]) for n, w in (("bvB", D), ("boB", D), ("pbB", D), ("slB", H)))
        w1s = sb("w1s", [128, E * F])
        b1s = sb("b1s", [128, E * FC])
        b2s = sb("b2s", [E, D])
        keys_s, rw_s = sb("keys_s", [128, E]), sb("rw_s", [128, E])
        rb_s = sb("rb_s", [1, E])

        kst = sb("kst", [128, B, PAIRS, CTX], bf16)
        kf = sb("kf", [128, CTX])
        kr = sb("kr", [128, CTX])
        kp = sb("kp", [128, 3, CTX], bf16)
        ksq = sb("ksq", [128, 512], bf16)
        kmx = sb("kmx", [H, B, NG])
        vau = sb("vau", [128, B * NK, H, DK + 1])
        qst = sb("qst", [128, B, PAIRS, 2, 128], bf16)
        qf = sb("qf", [128, B * S])
        qr = sb("qr", [128, B * S])
        qp = sb("qp", [128, 3, B * S], bf16)
        NE = 4
        ex = sb("ex", [128, NE, 512])
        mx2 = sb("mx2", [128, B, H, 2])
        mx = sb("mx", [128, B, H])
        ngm = sb("ngm", [128, GH])
        ngr = sb("ngr", [128, GH])
        mpad = sb("mpad", [128, 2, GH // 2, 128], bf16)
        oS = sb("oS", [128, B, 512])
        zero = sb("zero", [128, 8])
        expo = sb("expo", [128, 64])
        st = sb("st", [128, B, 6])
        mv = sb("mv", [128, B, 2])
        rstd = sb("rstd", [128, B])
        xn = sb("xn", [128, B, D])
        xT = sb("xT", [128, B * S])
        rec = sb("rec", [128, B, H])
        cn = sb("cn", [128, B, D])
        cnT = sb("cnT", [128, B * S])
        qsq = sb("qsq", [128, B * S])
        blbk = sb("blbk", [128, H])
        kmaxc = sb("kmaxc", [H, B])
        kbc = sb("kbc", [H, B, 128])
        count = sb("count", [128, 1])
        fk = sb("fk", [128, 2, 128], bf16)
        fq = sb("fq", [128, 2, 256], bf16)
        fv = sb("fv", [128, GH, DK + 1])
        fo = sb("fo", [128, 128])
        facc = sb("facc", [128, 128])
        sm = sb("sm", [128, B, H])
        sl8 = sb("sl8", [128, H])
        qT = sb("qT", [128, B, 128])
        neg = sb("neg", [128, 128])
        gk = sb("gk", [128, E])
        ksq2 = sb("ksq2", [128, E])
        lg = sb("lg", [128, B, E])
        lmx = sb("lmx", [128, B])
        rk = sb("rk", [128, B, E])
        wr = sb("wr", [128, B, E])
        wsum = sb("wsum", [128, B])
        wT = sb("wT", [E, B * S])
        nrm = sb("nrm", [128, B, H])
        qbk = sb("qbk", [128, B, H])
        sumq = sb("sumq", [128, B, H])
        low = sb("low", [128, B, H])
        bad = sb("bad", [128, 1])
        onec = sb("onec", [128, 128])
        flag = sb("flag", [1, 1], i32)

        parts_d = nc.dram_tensor("parts_d", [B, 3, 128, CTX], bf16).ap()
        qparts_d = nc.dram_tensor("qparts_d", [3, 128, B * S], bf16).ap()

        kflat = kst[:].rearrange("p b r k -> p (b r k)").bitcast(fp32)
        w2s = kflat[:, 0:E * FC * D].rearrange("p (n d) -> p n d", d=D)
        sc = [kflat[:, 10240 + 2048 * i:12288 + 2048 * i].rearrange("p (h k) -> p h k", h=H) for i in range(B)]
        pT = [cT[:, b, :].rearrange("p (h k) -> p h k", h=H) for b in range(B)]
        cflat = cT[:].rearrange("p b k -> p (b k)")
        rope = [kflat[:, 8192 + 512 * n:8704 + 512 * n].rearrange("p (b n) -> p b n", b=B) for n in range(3)]
        rankw = [kflat[:, 10240 + 512 * n:10752 + 512 * n].rearrange("p (b e f) -> p b e f", b=B, e=E) for n in range(2)]
        kq = ex[:, 0:B, :].rearrange("p b (h k) -> p b h k", h=GH)
        xsq = qsq
        yT = kflat[:, 12288:12544]
        fe, fC = kr[:, 0:512], kr[:, 512:1024]
        alibi = kf[:].rearrange("p (h k) -> p h k", h=H)
        hid = [cflat[:, 1024 * i:1024 * (i + 1)].rearrange("p (f t) -> p f t", f=FC) for i in range(4)]

        ps = es.enter_context(nc.psum_tensor("ps", [128, 8, 512], fp32))

        d_x, d_w, d_c, d_k, d_q, d_wt, d_w2, d_out, d_const = (sem("d_" + n) for n in (
            "x", "w", "c", "k", "q", "wt", "w2", "out", "const"))
        d_kb = [sem(f"d_kb{b}") for b in range(B)]
        d_kd = [sem(f"d_kd{b}") for b in range(B)]
        d_qd = sem("d_qd")
        d_fg, d_fc, d_fs = sem("d_fg"), sem("d_fc"), sem("d_fs")
        s = {n: sem("s_" + n) for n in (
            "dve", "pool", "act", "pe", "init", "rstd", "xn", "xT", "xTc", "q", "qf", "qparts", "kproj", "kfe", "kcast", "kr", "kparts",
            "ksq", "kn", "kmx", "v", "vau", "unitA", "redA", "mpad", "mT", "mrow", "scB", "exp", "pv",
            "blk", "nrm", "redn", "lowa", "okc", "tab", "alibi", "qkv", "rope", "qkT", "qkTc", "s2", "sc2", "ex2", "pT", "pTd", "pTa",
            "pv2", "cn2", "gprep", "lgt", "lgs", "rex", "wts", "wTp", "wTc", "up", "gelu", "wb", "mul", "down", "y", "yc", "yt",
            "f_C", "f_Cc", "f_sc", "f_ex", "f_max", "f_pv", "f_add", "f_end", "f_clr",
            "oS", "oT", "bnd", "low", "cnt", "flag", "cn", "cnT", "cnTc", "o", "x1")}

        block = es.enter_context(nc.Block())

        def units():
            return [(8 * g + 2 * j + f, g // NG, GH * (g % NG) + j, f)
                    for g in range(B * NG) for j in range(GH) for f in range(2)]

        UNITS = units()
        N_CONST = 16
        LEAD = 2

        kst_v = kst[:].rearrange("p b r k -> p (b r) k")
        qst_v = qst[:].rearrange("p b r a n -> p (b r) (a n)")
        vau_v = vau[:].rearrange("p c h d -> p (c h) d")
        oS_v = oS[:].rearrange("p b n -> p (b n)")

        def bad_rows(eng):
            eng.wait_ge(s["flag"], 1)
            return eng.value_load(flag[0:1, 0:1], min_val=0, max_val=128)

        def clip_moves(sp):
            with sp.If(bad_rows(sp)):
                with sp.Fori(0, B) as b:
                    with sp.Fori(0, NG) as n:
                        g = b * NG + n
                        sp.dma_start(fq[:], qst_v[:, bass.ds(2 * g, 2), :]).then_inc(d_fg, 16)
                        sp.dma_start(fo[:], oS_v[:, bass.ds(128 * g, 128)]).then_inc(d_fg, 16)
                        with sp.Fori(0, NK) as c:
                            it = g * NK + c
                            sp.wait_ge(s["f_pv"], it + 1)
                            sp.dma_start(fk[:], kst_v[:, bass.ds(2 * g, 2), bass.ds(128 * c, 128)]).then_inc(d_fc, 16)
                            sp.dma_start(fv[:], vau_v[:, bass.ds((b * NK + c) * H + n * GH, GH), :]).then_inc(d_fc, 16)
                        sp.wait_ge(s["f_add"], (g + 1) * NK)
                        sp.dma_start(oS_v[:, bass.ds(128 * g, 128)], facc[:]).then_inc(d_fs, 16)
                sp.wait_ge(d_fs, B * NG * 16)
                sp.wait_ge(s["f_end"], 1)

        @block.sync
        def _(sp):
            sp.dma_start(xs[:], x.rearrange("b s d -> s b d")).then_inc(d_x, 16)
            sp.dma_start(ident[:], ident_in).then_inc(d_x, 16)
            sp.dma_start(wks[:], wk).then_inc(d_w, 16)
            sp.dma_start(cols[:, 0:1], bq).then_inc(d_w, 16)
            sp.dma_start(cols[:, 1:2], bk).then_inc(d_w, 16)
            sp.dma_start(cT[:, 0, :], ctxT[0]).then_inc(d_c, 16)
            sp.dma_start(wqs[:], wq).then_inc(d_w, 16)
            sp.dma_start(blocks[:], blocks_in).then_inc(d_w, 16)
            sp.dma_start(wvs[:], wv).then_inc(d_w, 16)
            sp.dma_start(bvB[:], bv.broadcast_to([128, D])).then_inc(d_w, 16)
            sp.dma_start(cT[:, 1, :], ctxT[1]).then_inc(d_c, 16)
            for a in range(2):
                sp.dma_start(kst_v[HALF * a:HALF * a + TERM0, :, :].bitcast(i32),
                             ones_in.unsqueeze(1).broadcast_to([TERM0, B * PAIRS, CTX // 2])).then_inc(d_k, 16)
            sp.wait_ge(s["qparts"], 1)
            sp.dma_start(qparts_d.rearrange("t r n -> r t n"), qp[:]).then_inc(d_qd, 16)
            sp.wait_ge(s["init"], 1)
            sp.wait_ge(d_qd, 16)
            for a in range(2):
                for t, (tq, _) in enumerate(TERMS):
                    r0 = HALF * a + TERM0 + DK * t
                    src = qparts_d[tq].rearrange("(p a d) (b n) -> a d b p n", a=2, d=DK, b=B)[a]
                    for b in range(B):
                        sp.dma_start(qst[r0:r0 + DK, b, :, a, :], src[:, b]).then_inc(d_q, 16)
            for b in range(B):
                sp.wait_ge(s["kparts"], b + 1)
                sp.dma_start(parts_d[b].rearrange("t r n -> r t n"), kp[:]).then_inc(d_kd[b], 16)
                sp.wait_ge(d_kd[b], 16)
                for a in range(2):
                    for t, (_, tk) in enumerate(TERMS):
                        r0 = HALF * a + TERM0 + DK * t
                        src = parts_d[b, tk].rearrange("(p a d) n -> a d p n", a=2, d=DK)[a]
                        sp.dma_start(kst[r0:r0 + DK, b, :, :], src).then_inc(d_kb[b], 16)
            for dst, src in ((wos[:], wo), (boB[:], bo.broadcast_to([128, D])), (qkvs[:], qkvw), (projs[:], projw),
                             (pbB[:], projb.broadcast_to([128, D])), (slB[:], slopes.broadcast_to([128, H])),
                             (rot[:], rot_in), (dist[:], dist_in), (tri[:], tri_in), (quart[:], quart_in), (sumrow[:], sumrow_in),
                             (b1s[:], b1), (b2s[:], b2), (keys_s[:], keysT), (rw_s[:], rwT), (rb_s[:], rb)):
                sp.dma_start(dst, src).then_inc(d_const, 16)
            for n in range(4):
                sp.dma_start(w1s[:, n * E * F // 4:(n + 1) * E * F // 4], w1[:, n * E * F // 4:(n + 1) * E * F // 4])\
                    .then_inc(d_wt, 16)
            clip_moves(sp)
            sp.wait_ge(s["scB"], B * NG * NK)
            for n in range(4):
                sp.dma_start(w2s[:, 16 * n:16 * n + 16, :], w2[:, 16 * n:16 * n + 16, :]).then_inc(d_w2, 16)
            sp.wait_ge(s["x1"], 1)
            sp.dma_start(out.rearrange("b s d -> s b d"), xs[:]).then_inc(d_out, 16)
            sp.wait_ge(d_out, 16)

        @block.gpsimd
        def _(pool):
            chain = [0]

            def link(ins):
                chain[0] += 1
                ins.then_inc(s["pool"], 1)
                pool.wait_ge(s["pool"], chain[0])

            link(pool.memset(expo[:, 0:B], -0.5))
            link(pool.memset(expo[:, 32:64], 0.5))
            link(pool.memset(qst[:].bitcast(i32), 0))
            pool.sem_inc(s["init"], 1)
            link(pool.memset(onec[:], 1.0))
            link(pool.memset(mpad[:].bitcast(i32), 0))
            link(pool.memset(oS[:], 0.0))
            link(pool.memset(vau[:, :, :, DK:DK + 1], 1.0))
            pool.sem_inc(s["init"], 1)

            def rstds(n):
                pool.wait_ge(s["rstd"], 2 * n + 1)
                pool.tensor_tensor(rstd[:], rstd[:], expo[:, 0:B], ALU.pow).then_inc(s["rstd"], 1)

            rstds(0)
            pool.wait_ge(s["nrm"], 1)
            n32 = nrm[:].rearrange("p b h -> p (b h)")
            pool.tensor_tensor(n32, n32, expo[:, 32:64], ALU.pow).then_inc(s["nrm"], 1)
            pool.wait_ge(d_const, 16 * N_CONST)
            link(pool.tensor_scalar(sl8[:], slB[:], MAX_BIAS, None, ALU.mult))
            pool.wait_ge(s["kparts"], B)
            link(pool.tensor_tensor(alibi, dist[:].unsqueeze(1).broadcast_to([128, H, 128]),
                                    sl8[:].unsqueeze(2).broadcast_to([128, H, 128]), ALU.mult))
            link(pool.memset(neg[:], -1.0))
            link(pool.tensor_scalar(gk[:], keys_s[:], 2.0, None, ALU.mult))
            link(pool.tensor_tensor(gk[:], gk[:], rw_s[:], ALU.add))
            link(pool.tensor_tensor(ksq2[:], keys_s[:], keys_s[:], ALU.mult))
            pool.sem_inc(s["tab"], 1)
            rstds(1)
            rstds(2)

        @block.vector
        def _(dve):
            chain = [0]

            def link(ins):
                chain[0] += 1
                ins.then_inc(s["dve"], 1)
                dve.wait_ge(s["dve"], chain[0])

            def layer_norm(n):
                for b in range(B):
                    last = dve.bn_stats(st[:, b, :], xs[:, b, :])
                link(last)
                for b in range(B):
                    last = dve.bn_aggr(mv[:, b, :], st[:, b, :])
                link(last)
                dve.tensor_scalar(rstd[:], mv[:, :, 1], LN_EPS, None, ALU.add).then_inc(s["rstd"], 1)
                dve.wait_ge(s["rstd"], 2 * n + 2)
                for b in range(B):
                    last = dve.tensor_scalar(xn[:, b, :], xs[:, b, :], mv[:, b, 0:1], rstd[:, b:b + 1],
                                             ALU.subtract, ALU.mult)
                last.then_inc(s["xn"], 1)
                dve.wait_ge(s["xT"], n + 1)
                dve.tensor_copy(xT[:], ps[:, 7, 0:B * S]).then_inc(s["xTc"], 1)

            dve.wait_ge(d_x, 32)
            link(dve.tensor_copy(identb[:], ident[:]))
            layer_norm(0)
            dve.wait_ge(d_w, 16 * 7)
            dve.tensor_copy(blocksb[:], blocks[:]).then_inc(s["blk"], 1)
            dve.wait_ge(s["q"], 1)
            link(dve.tensor_scalar(qf[:], ps[:, 7, 0:B * S], cols[:, 0:1], None, ALU.add))
            link(dve.tensor_copy(qp[:, 0, :], qf[:]))
            link(dve.tensor_tensor(qr[:], qf[:], qp[:, 0, :], ALU.subtract))
            link(dve.tensor_copy(qp[:, 1, :], qr[:]))
            dve.tensor_tensor(qp[:, 2, :], qr[:], qp[:, 1, :], ALU.subtract).then_inc(s["qparts"], 1)
            for b in range(B):
                for n in range(NG):
                    dve.wait_ge(s["kn"], NG * b + n + 1)
                    last = dve.tensor_reduce(out=kmx[:, b, n:n + 1], in_=ps[0:H, 6, :], axis=AX.X, op=ALU.max)
                    last.then_inc(s["kmx"], 1)
                if b:
                    dve.wait_ge(d_kd[b - 1], 16)
                dve.wait_ge(s["kfe"], NG * (b + 1))
                link(dve.tensor_copy(kp[:, 0, :], kf[:]))
                link(dve.tensor_tensor(kr[:], kf[:], kp[:, 0, :], ALU.subtract))
                dve.sem_inc(s["kr"], 1)
                link(dve.tensor_copy(kp[:, 1, :], kr[:]))
                dve.tensor_tensor(kp[:, 2, :], kr[:], kp[:, 1, :], ALU.subtract).then_inc(s["kparts"], 1)
            for n in range(B * NK // 4):
                dve.wait_ge(s["v"], n + 1)
                dve.tensor_tensor(vau[:, 4 * n:4 * n + 4, :, 0:DK],
                                  ps[:, 4 + n % 2, :].rearrange("p (c h d) -> p c h d", c=4, h=H),
                                  bvB[:].rearrange("p (h d) -> p h d", h=H).unsqueeze(1).broadcast_to([128, 4, H, DK]),
                                  ALU.add).then_inc(s["vau"], 1)

            link(dve.tensor_tensor(qsq[:], qf[:], qf[:], ALU.mult))
            link(dve.tensor_scalar(blbk[:], blocks[:], cols[:, 1:2], None, ALU.mult))
            dve.wait_ge(s["kmx"], B * NG)
            link(dve.tensor_reduce(out=kmaxc[:], in_=kmx[:], axis=AX.X, op=ALU.max))
            dve.tensor_scalar(kbc[:], kmaxc[:].unsqueeze(2).broadcast_to([H, B, 128]), 1.02, None, ALU.mult)\
                .then_inc(s["bnd"], 1)
            dve.wait_ge(s["bnd"], 2)
            bnd = ps[:, 7, 256:256 + 3 * B * H].rearrange("p (b t h) -> p b t h", b=B, t=3)
            link(dve.tensor_copy(sumq[:], bnd[:, :, 0, :]))
            link(dve.tensor_copy(qbk[:], bnd[:, :, 2, :]))
            dve.tensor_tensor(nrm[:], sumq[:], bnd[:, :, 1, :], ALU.mult).then_inc(s["nrm"], 1)
            dve.wait_ge(s["nrm"], 2)
            link(dve.tensor_tensor(low[:], qbk[:], nrm[:], ALU.subtract))

            def maxima(n):
                u, b, h, f = UNITS[n]
                dve.wait_ge(s["unitA"], u + 1)
                dve.tensor_reduce(out=mx2[:, b, h, f:f + 1],
                                  in_=ps[:, 2 * (u % 2):2 * (u % 2) + 2, :].rearrange("p a k -> p (a k)"),
                                  axis=AX.X, op=ALU.max).then_inc(s["redA"], 1)
                if u % 8 == 7:
                    g = u // 8
                    hs = slice(GH * (g % NG), GH * (g % NG) + GH)
                    dve.wait_ge(s["redA"], u + 1)
                    link(dve.tensor_tensor(mx[:, b, hs], mx2[:, b, hs, 0], mx2[:, b, hs, 1], ALU.max))
                    link(dve.tensor_scalar(ngm[:], mx[:, b, hs], -1.0, None, ALU.mult))
                    m = mpad[:, g % 2].rearrange("p r (a c) -> p (r a) c", a=2)
                    link(dve.tensor_copy(m[:, :, 0], ngm[:]))
                    link(dve.tensor_tensor(ngr[:], ngm[:], m[:, :, 0], ALU.subtract))
                    link(dve.tensor_copy(m[:, :, 1], ngr[:]))
                    dve.tensor_tensor(m[:, :, 2], ngr[:], m[:, :, 1], ALU.subtract).then_inc(s["mpad"], 1)

            def rows(g):
                b, r = g // NG, 2 * (g % NG)
                dve.wait_ge(s["mT"], g + 1)
                for a in range(2):
                    last = dve.tensor_copy(
                        qst[HALF * a:HALF * a + M_ROWS, b, r:r + 2, a, :],
                        ps[HALF * a:HALF * a + M_ROWS, 7, 0:128].bitcast(bf16).rearrange("p (r n) -> p r n", r=2))
                last.then_inc(s["mrow"], 1)

            def sums(b):
                dve.wait_ge(s["pv"], NK * NG * (b + 1))
                for g in range(GH):
                    last = dve.tensor_copy(oS[32 * g:32 * g + DK + 1, b, :], ps[32 * g:32 * g + DK + 1, 6, :])
                last.then_inc(s["oS"], 1)

            for n in range(len(UNITS)):
                maxima(n)
                if n % 8 == 0 and n:
                    rows(n // 8 - 1)
                if n == 8 * NG + 8 + LEAD - 1:
                    sums(0)
            rows(B * NG - 1)
            sums(B - 1)
            link(dve.tensor_tensor(low[:], low[:], mx[:], ALU.subtract))
            dve.sem_inc(s["lowa"], 1)
            for b in range(B):
                dve.wait_ge(s["oT"], b + 1)
                link(dve.tensor_copy(sumq[:, b, :].rearrange("p (n g) -> p n g", n=NG),
                                     ps[:, 4 + b, :].rearrange("p (n g c) -> p n g c", n=NG, g=GH)[:, :, :, DK]))
            dve.wait_ge(s["okc"], 1)
            link(dve.scalar_tensor_tensor(out=qbk[:], in0=sumq[:], scalar=1.01 * CLIP, in1=nrm[:], op0=ALU.mult, op1=ALU.is_le))
            dve.tensor_reduce(out=count[:], in_=qbk[:].rearrange("p b h -> p (b h)"), axis=AX.X, op=ALU.min)\
                .then_inc(s["cnt"], 1)
            dve.wait_ge(s["cnt"], 2)
            dve.tensor_scalar(flag[:], ps[0:1, 7, 0:1], -1.0, 128.0, ALU.mult, ALU.add).then_inc(s["flag"], 1)
            with dve.If(bad_rows(dve)):
                dve.memset(facc[:], 0.0).then_inc(s["f_clr"], 1)
                with dve.Fori(0, B) as b:
                    with dve.Fori(0, NG) as n:
                        g = b * NG + n
                        dve.wait_ge(s["f_C"], g + 1)
                        dve.tensor_scalar(fC, ps[:, 2, :], CLIP, None, ALU.mult).then_inc(s["f_Cc"], 1)
                        with dve.Fori(0, NK) as c:
                            it = g * NK + c
                            dve.wait_ge(s["f_Cc"], g + 1)
                            dve.wait_ge(s["f_clr"], g + 1)
                            dve.wait_ge(s["f_ex"], it + 1)
                            dve.tensor_tensor(fe, fe, fC, ALU.max).then_inc(s["f_max"], 1)
                            dve.wait_ge(s["f_pv"], it + 2)
                            for j in range(GH):
                                q = slice(32 * j, 32 * j + DK + 1)
                                last = dve.tensor_tensor(facc[q, :], facc[q, :], ps[q, 1, 0:128], ALU.add)
                            last.then_inc(s["f_add"], 1)
                            dve.wait_ge(s["f_add"], it + 1)
                        dve.wait_ge(d_fs, (g + 1) * 16)
                        dve.memset(facc[:], 0.0).then_inc(s["f_clr"], 1)
                dve.wait_ge(s["f_end"], 1)
            for b in range(B):
                o = ps[:, 4 + b, :].rearrange("p (n g c) -> p n g c", n=NG, g=GH)
                r4 = rec[:, b, :].rearrange("p (n g) -> p n g", n=NG)
                link(dve.reciprocal(r4, o[:, :, :, DK]))
                dve.tensor_tensor(cn[:, b, :].rearrange("p (n g d) -> p n g d", n=NG, g=GH), o[:, :, :, 0:DK],
                                  r4.unsqueeze(3).broadcast_to([128, NG, GH, DK]), ALU.mult).then_inc(s["cn"], 1)
            dve.wait_ge(s["cnT"], 1)
            dve.tensor_copy(cnT[:], ps[:, 7, 0:B * S]).then_inc(s["cnTc"], 1)
            dve.wait_ge(s["o"], 1)
            dve.wait_ge(d_const, 16 * N_CONST)
            link(dve.tensor_tensor(xs[:], xs[:], boB[:].unsqueeze(1).broadcast_to([128, B, D]), ALU.add))
            link(dve.tensor_tensor(xs[:], xs[:], ps[:, 6, 0:B * D].rearrange("p (b d) -> p b d", b=B), ALU.add))

            layer_norm(1)
            for b in range(B):
                dve.wait_ge(s["qkv"], b + 1)
                qk = ps[:, 4 + b, 0:2 * D].rearrange("p (h a d) -> p h a d", h=2 * H, a=2)
                t, u, r = (rope[n][:, b, :].rearrange("p (h a d) -> p h a d", h=2 * H, a=2) for n in range(3))
                cs, sn = (rot[:, n, :].rearrange("p (a d) -> p a d", a=2) for n in range(2))
                h2 = [128, 2 * H, DK // 2]
                for a in range(2):
                    dve.tensor_tensor(t[:, :, a], qk[:, :, a], cs[:, a].unsqueeze(1).broadcast_to(h2), ALU.mult)
                    last = dve.tensor_tensor(u[:, :, a], qk[:, :, 1 - a], sn[:, a].unsqueeze(1).broadcast_to(h2), ALU.mult)
                link(last)
                dve.tensor_tensor(rope[2][:, b, :], rope[0][:, b, :], rope[1][:, b, :], ALU.add).then_inc(s["rope"], 1)
                last = dve.tensor_copy(vau[:, b, :, 0:DK], ps[:, 4 + b, 2 * D:3 * D].rearrange("p (h d) -> p h d", h=H))
            link(last)
            for b in range(B):
                dve.wait_ge(s["qkT"], b + 1)
                dve.tensor_copy(qT[:, b, :], ps[:, 6 + b, 0:128])
                dve.tensor_tensor(kq[:, b], ps[:, 6 + b, 128:256].unsqueeze(1).broadcast_to([128, GH, 128]),
                                  quart[:].unsqueeze(2).broadcast_to([128, GH, 128]), ALU.mult).then_inc(s["qkTc"], 1)
            dve.wait_ge(s["tab"], 1)
            for b in range(B):
                dve.wait_ge(s["s2"], b + 1)
                link(dve.scalar_tensor_tensor(out=sc[b].rearrange("p h k -> p (h k)"),
                                              in0=ps[:, 4 * b:4 * b + 4, :].rearrange("p a n -> p (a n)"), scalar=SCALE,
                                              in1=alibi.rearrange("p h k -> p (h k)"), op0=ALU.mult, op1=ALU.add))
                link(dve.tensor_reduce(out=sm[:, b, :], in_=sc[b], axis=AX.X, op=ALU.max))
                dve.tensor_tensor(sc[b], sc[b], sm[:, b, :].unsqueeze(2).broadcast_to([128, H, 128]), ALU.subtract)\
                    .then_inc(s["sc2"], 1)
            for b in range(B):
                for n in (0, 2):
                    dve.wait_ge(s["pT"], 4 * b + n + 1)
                    dve.tensor_copy(pT[b][:, 4 * n:4 * n + 4, :], ps[:, 4 * b + n, :].rearrange("p (h k) -> p h k", h=4))\
                        .then_inc(s["pTd"], 1)
                dve.wait_ge(s["pv2"], b + 1)
                o = ps[:, 4 * b, 0:H * (DK + 1)].rearrange("p (h c) -> p h c", h=H)
                link(dve.reciprocal(rec[:, b, :], o[:, :, DK]))
                dve.tensor_tensor(cn[:, b, :].rearrange("p (h d) -> p h d", h=H), o[:, :, 0:DK],
                                  rec[:, b, :].unsqueeze(2).broadcast_to([128, H, DK]), ALU.mult).then_inc(s["cn"], 1)
            dve.wait_ge(s["cnT"], 2)
            dve.tensor_copy(cnT[:], ps[:, 1, 0:B * S]).then_inc(s["cnTc"], 1)
            link(dve.tensor_tensor(xs[:], xs[:], pbB[:].unsqueeze(1).broadcast_to([128, B, D]), ALU.add))
            dve.wait_ge(s["o"], 2)
            link(dve.tensor_tensor(xs[:], xs[:], ps[:, 2, 0:B * D].rearrange("p (b d) -> p b d", b=B), ALU.add))

            layer_norm(2)
            dve.wait_ge(s["xTc"], 3)
            dve.tensor_tensor(xsq[:], xT[:], xT[:], ALU.mult).then_inc(s["lgs"], 1)
            dve.wait_ge(s["lgt"], 1)
            link(dve.tensor_copy(lg[:], ps[:, 7, 256:256 + B * E].rearrange("p (b e) -> p b e", b=B)))
            link(dve.tensor_reduce(out=lmx[:], in_=lg[:], axis=AX.X, op=ALU.max))
            dve.tensor_tensor(wr[:], lg[:], lmx[:].unsqueeze(2).broadcast_to([128, B, E]), ALU.subtract).then_inc(s["rex"], 1)
            gt, eq = rankw
            for b in range(B):
                f_ = lg[:, b].unsqueeze(1).broadcast_to([128, E, E])
                e_ = lg[:, b].unsqueeze(2).broadcast_to([128, E, E])
                dve.tensor_tensor(gt[:, b], f_, e_, ALU.is_gt)
                last = dve.tensor_tensor(eq[:, b], f_, e_, ALU.is_equal)
            link(last)
            for b in range(B):
                last = dve.tensor_tensor(eq[:, b], eq[:, b], tri[:], ALU.mult)
            link(last)
            link(dve.tensor_tensor(gt.rearrange("p b e f -> p (b e f)"), gt.rearrange("p b e f -> p (b e f)"),
                                   eq.rearrange("p b e f -> p (b e f)"), ALU.add))
            link(dve.tensor_reduce(out=rk[:], in_=gt, axis=AX.X, op=ALU.add))
            dve.wait_ge(s["rex"], 2)
            link(dve.scalar_tensor_tensor(out=wr[:], in0=rk[:], scalar=TOP - 0.5, in1=wr[:], op0=ALU.is_lt, op1=ALU.mult))
            link(dve.tensor_reduce(out=wsum[:], in_=wr[:], axis=AX.X, op=ALU.add))
            link(dve.reciprocal(wsum[:], wsum[:]))
            dve.tensor_tensor(wr[:], wr[:], wsum[:].unsqueeze(2).broadcast_to([128, B, E]), ALU.mult).then_inc(s["wts"], 1)
            dve.wait_ge(s["wTp"], 1)
            dve.tensor_copy(wT[:], ps[0:E, 7, 0:B * S]).then_inc(s["wTc"], 1)
            for e in range(E):
                dve.wait_ge(s["gelu"], FC * (e + 1))
                dve.wait_ge(s["wb"], e + 1)
                dve.tensor_tensor(hid[e % 4], hid[e % 4],
                                  ps[:, 4 + e % 2, 0:B * S].unsqueeze(1).broadcast_to([128, FC, B * S]), ALU.mult)\
                    .then_inc(s["mul"], 1)
            dve.wait_ge(s["y"], 1)
            dve.tensor_copy(yT, ps[:, 6, 0:B * S]).then_inc(s["yc"], 1)
            dve.wait_ge(s["yt"], 1)
            dve.tensor_tensor(xs[:], xs[:], ps[:, 7, 0:B * D].rearrange("p (b d) -> p b d", b=B), ALU.add).then_inc(s["x1"], 1)

        @block.scalar
        def _(act):
            act.wait_ge(d_w, 16 * 7)
            for b in range(B):
                if b:
                    act.wait_ge(s["kr"], b)
                for n in range(NG):
                    u = NG * b + n
                    act.wait_ge(s["kproj"], u + 1)
                    if u:
                        act.wait_ge(s["kn"], u)
                    act.activation(ksq[:], ps[:, u % 4, :], ACT.Square).then_inc(s["ksq"], 1)
                    act.activation(kf[:, 512 * n:512 * n + 512], ps[:, u % 4, :], ACT.Identity,
                                   bias=cols[:, 1:2]).then_inc(s["kfe"], 1)
            for g in range(B * NG):
                for c in range(NK):
                    n = NK * g + c
                    act.wait_ge(s["scB"], n + 1)
                    if n >= NE:
                        act.wait_ge(s["pv"], n - NE + 1)
                    act.activation(ex[:, n % NE, :], ps[:, 4 + n % 2, :], ACT.Exp, scale=SCALE).then_inc(s["exp"], 1)
            act.wait_ge(s["lowa"], 1)
            act.activation(nrm[:], low[:], ACT.Exp, scale=SCALE).then_inc(s["okc"], 1)
            with act.If(bad_rows(act)):
                with act.Fori(0, B * NG * NK) as it:
                    act.wait_ge(s["f_sc"], it + 1)
                    act.activation(fe, ps[:, 0, :], ACT.Exp, scale=SCALE).then_inc(s["f_ex"], 1)
            for b in range(B):
                act.wait_ge(s["sc2"], b + 1)
                act.activation(sc[b], sc[b], ACT.Exp).then_inc(s["ex2"], 1)
                for n in (1, 3):
                    act.wait_ge(s["pT"], 4 * b + n + 1)
                    act.activation(pT[b][:, 4 * n:4 * n + 4, :], ps[:, 4 * b + n, :].rearrange("p (h k) -> p h k", h=4),
                                   ACT.Copy).then_inc(s["pTa"], 1)
            act.wait_ge(s["rex"], 1)
            act.activation(wr[:], wr[:], ACT.Exp).then_inc(s["rex"], 1)
            for e in range(E):
                if e >= 4:
                    act.wait_ge(s["down"], e - 3)
                for n in range(FC):
                    act.wait_ge(s["up"], 2 * e + n // 2 + 1)
                    act.activation(hid[e % 4][:, n, :], ps[:, (2 * e + n // 2) % 4, 256 * (n % 2):256 * (n % 2) + 256], ACT.Gelu,
                                   bias=b1s[:, FC * e + n:FC * e + n + 1]).then_inc(s["gelu"], 1)

        @block.tensor
        def _(pe):
            pe.wait_ge(s["xn"], 1)
            for b in range(B):
                last = pe.transpose(ps[:, 7, b * S:(b + 1) * S], xn[:, b, :], ident[:])
            last.then_inc(s["xT"], 1)
            pe.wait_ge(s["xTc"], 1)
            pe.wait_ge(d_w, 16 * 7)
            pe.matmul(ps[:, 7, 0:B * S], wqs[:], xT[:], start=True, stop=True).then_inc(s["q"], 1)

            def norms(u):
                pe.wait_ge(s["ksq"], u + 1)
                if u == 0:
                    pe.wait_ge(s["blk"], 1)
                if u:
                    pe.wait_ge(s["kmx"], u)
                pe.matmul(ps[0:H, 6, :], blocksb[:], ksq[:], start=True, stop=True).then_inc(s["kn"], 1)

            for b in range(B):
                pe.wait_ge(d_c, 16 * B)
                for n in range(NG):
                    u = NG * b + n
                    if u >= 4:
                        pe.wait_ge(s["kfe"], u - 3)
                    pe.matmul(ps[:, u % 4, :], wks[:], cT[:, b, 512 * n:512 * n + 512], start=True, stop=True)\
                        .then_inc(s["kproj"], 1)
                    if u:
                        norms(u - 1)
            norms(B * NG - 1)
            cTf = cT[:].rearrange("p b k -> p (b k)")
            for n in range(B * NK // 4):
                if n >= 2:
                    pe.wait_ge(s["vau"], n - 1)
                for j in range(4):
                    c = 4 * n + j
                    last = pe.matmul(ps[:, 4 + n % 2, 128 * j:128 * j + 128], cTf[:, 128 * c:128 * c + 128], wvs[:],
                                     start=True, stop=True)
                last.then_inc(s["v"], 1)

            pe.wait_ge(s["bnd"], 1)
            for b in range(B):
                c0 = 256 + 3 * H * b
                pe.matmul(ps[:, 7, c0:c0 + H], qsq[:, b * S:(b + 1) * S], blocks[:], start=True, stop=True)
                pe.matmul(ps[:, 7, c0 + H:c0 + 2 * H], kbc[:, b, :], ident[0:H, 0:H], start=True, stop=True)
                last = pe.matmul(ps[:, 7, c0 + 2 * H:c0 + 3 * H], qf[:, b * S:(b + 1) * S], blbk[:], start=True, stop=True)
            last.then_inc(s["bnd"], 1)

            def unit(n):
                u, b, h, f = UNITS[n]
                if u == 0:
                    pe.wait_ge(d_q, 16 * 2 * B * len(TERMS))
                    pe.wait_ge(s["kfe"], NG * B)
                    pe.wait_ge(d_k, 32)
                if u % 32 == 0:
                    pe.wait_ge(d_kb[b], 16 * 2 * len(TERMS))
                if u >= 2:
                    pe.wait_ge(s["redA"], u - 1)
                for j in range(2):
                    k0 = 1024 * f + 512 * j
                    last = pe.matmul(ps[:, 2 * (u % 2) + j, :], qst[:, b, h // 2, h % 2, :],
                                     kst[:, b, h // 2, k0:k0 + 512], start=True, stop=True)
                last.then_inc(s["unitA"], 1)

            def turn(g):
                pe.wait_ge(s["mpad"], g + 1)
                if g:
                    pe.wait_ge(s["mrow"], g)
                for r in range(2):
                    last = pe.transpose(ps[:, 7, 64 * r:64 * r + 64].bitcast(bf16), mpad[:, g % 2, r, :], identb[:])
                last.then_inc(s["mT"], 1)

            def scores(g, c):
                b, r = g // NG, 2 * (g % NG)
                n = NK * g + c
                if c == 0:
                    pe.wait_ge(s["mrow"], g + 1)
                if n == 0:
                    pe.wait_ge(s["vau"], B * NK // 4)
                if n >= 2:
                    pe.wait_ge(s["exp"], n - 1)
                for j in range(2):
                    last = pe.matmul(ps[:, 4 + n % 2, 256 * j:256 * j + 256], kst[:, b, r + j, 128 * c:128 * c + 128],
                                     qst[:, b, r + j, :, :].rearrange("p a n -> p (a n)"), start=True, stop=True)
                last.then_inc(s["scB"], 1)

            def values(g, c):
                b, hg = g // NG, g % NG
                n = NK * g + c
                pe.wait_ge(s["exp"], n + 1)
                if n == NK * NG:
                    pe.wait_ge(s["oS"], 1)
                for j in range(GH):
                    last = pe.matmul(ps[32 * j:32 * j + DK + 1, 6, 128 * hg:128 * hg + 128],
                                     vau[:, NK * b + c, GH * hg + j, :], ex[:, n % NE, 128 * j:128 * j + 128],
                                     start=(c == 0), stop=(c == NK - 1), tile_position=(0, 32 * j))
                last.then_inc(s["pv"], 1)

            nu = 0

            def ahead(n):
                if n < len(UNITS):
                    unit(n)
                if n % 8 == 0 and n:
                    turn(n // 8 - 1)

            for nu in range(8 + LEAD):
                ahead(nu)
            nu = 8 + LEAD
            for g in range(B * NG):
                for c in range(NK):
                    scores(g, c)
                    if c % 2 == 0 and nu <= len(UNITS):
                        ahead(nu)
                        nu += 1
                    if c:
                        values(g, c - 1)
                    elif g:
                        values(g - 1, NK - 1)
            values(B * NG - 1, NK - 1)

            def turn_sums(b):
                for n in range(NG):
                    last = pe.transpose(ps[:, 4 + b, 128 * n:128 * n + 128], oS[:, b, 128 * n:128 * n + 128], ident[:])
                return last

            pe.wait_ge(s["exp"], B * NG * NK)
            for b in range(B):
                pe.wait_ge(s["oS"], b + 1)
                turn_sums(b).then_inc(s["oT"], 1)
            pe.wait_ge(s["cnt"], 1)
            pe.matmul(ps[0:1, 7, 0:1], count[:], onec[:, 0:1], start=True, stop=True).then_inc(s["cnt"], 1)
            with pe.If(bad_rows(pe)):
                pe.sem_inc(s["f_pv"], 1)
                with pe.Fori(0, B * NG) as g:
                    pe.wait_ge(d_fg, (g + 1) * 32)
                    for j in range(GH):
                        last = pe.matmul(ps[:, 2, 128 * j:128 * j + 128], sumrow[:, j:j + 1].broadcast_to([128, 128]), fo[:],
                                         start=True, stop=True)
                    last.then_inc(s["f_C"], 1)
                    with pe.Fori(0, NK) as c:
                        it = g * NK + c
                        pe.wait_ge(d_fc, (it + 1) * 32)
                        for j in range(2):
                            last = pe.matmul(ps[:, 0, 256 * j:256 * j + 256], fk[:, j, :], fq[:, j, :], start=True, stop=True)
                        last.then_inc(s["f_sc"], 1)
                        pe.wait_ge(s["f_max"], it + 1)
                        for j in range(GH):
                            last = pe.matmul(ps[32 * j:32 * j + DK + 1, 1, 0:128], fv[:, j, :], fe[:, 128 * j:128 * j + 128],
                                             start=True, stop=True, tile_position=(0, 32 * j))
                        last.then_inc(s["f_pv"], 1)
                        pe.wait_ge(s["f_add"], it + 1)
                pe.wait_ge(d_fs, B * NG * 16)
                turn_sums(0)
                turn_sums(1).then_inc(s["f_end"], 1)
            pe.wait_ge(s["cn"], B)
            for b in range(B):
                last = pe.transpose(ps[:, 7, b * S:(b + 1) * S], cn[:, b, :], ident[:])
            last.then_inc(s["cnT"], 1)
            pe.wait_ge(s["cnTc"], 1)
            pe.wait_ge(d_const, 16 * N_CONST)
            for b in range(B):
                last = pe.matmul(ps[:, 6, D * b:D * b + D], cnT[:, b * S:(b + 1) * S], wos[:], start=True, stop=True)
            last.then_inc(s["o"], 1)

            def turn_norm(n):
                pe.wait_ge(s["xn"], n + 1)
                for b in range(B):
                    last = pe.transpose(ps[:, 7, b * S:(b + 1) * S], xn[:, b, :], ident[:])
                last.then_inc(s["xT"], 1)
                pe.wait_ge(s["xTc"], n + 1)

            turn_norm(1)
            for b in range(B):
                pe.matmul(ps[:, 4 + b, 0:3 * D], xT[:, b * S:(b + 1) * S], qkvs[:], start=True, stop=True).then_inc(s["qkv"], 1)
            for b in range(B):
                pe.wait_ge(s["rope"], b + 1)
                for a in range(2):
                    last = pe.transpose(ps[:, 6 + b, 128 * a:128 * a + 128], rope[2][:, b, 128 * a:128 * a + 128], ident[:])
                last.then_inc(s["qkT"], 1)
            for b in range(B):
                pe.wait_ge(s["qkTc"], B if b else 1)
                for n in range(NG):
                    r = slice(32 * n, 32 * n + 32)
                    last = pe.matmul(ps[:, 4 * b + n, :], qT[r, b, :], kq[r, b].rearrange("p h k -> p (h k)"),
                                     start=True, stop=True, tile_position=(32 * n, 0))
                last.then_inc(s["s2"], 1)
            for b in range(B):
                pe.wait_ge(s["ex2"], b + 1)
                for n in range(NG):
                    for j in range(4):
                        last = pe.transpose(ps[:, 4 * b + n, 128 * j:128 * j + 128], sc[b][:, 4 * n + j, :], ident[:])
                    last.then_inc(s["pT"], 1)
                pe.wait_ge(s["pTd"], 2 * b + 2)
                pe.wait_ge(s["pTa"], 2 * b + 2)
                for h in range(H):
                    last = pe.matmul(ps[:, 4 * b, (DK + 1) * h:(DK + 1) * (h + 1)], pT[b][:, h, :], vau[:, b, h, :],
                                     start=True, stop=True)
                last.then_inc(s["pv2"], 1)
            pe.wait_ge(s["cn"], 2 * B)
            for b in range(B):
                last = pe.transpose(ps[:, 1, b * S:(b + 1) * S], cn[:, b, :], ident[:])
            last.then_inc(s["cnT"], 1)
            pe.wait_ge(s["cnTc"], 2)
            for b in range(B):
                last = pe.matmul(ps[:, 2, D * b:D * b + D], cnT[:, b * S:(b + 1) * S], projs[:], start=True, stop=True)
            last.then_inc(s["o"], 1)

            turn_norm(2)
            pe.wait_ge(s["lgs"], 1)
            pe.wait_ge(s["tab"], 1)
            for b in range(B):
                o = ps[:, 7, 256 + E * b:256 + E * (b + 1)]
                pe.matmul(o, xsq[:, b * S:(b + 1) * S], neg[:, 0:E], start=True, stop=False)
                pe.matmul(o, neg[:], ksq2[:], start=False, stop=False)
                pe.matmul(o, xT[:, b * S:(b + 1) * S], gk[:], start=False, stop=False)
                last = pe.matmul(o, onec[0:1, :], rb_s[:], start=False, stop=True)
            last.then_inc(s["lgt"], 1)

            def up(e):
                if e >= 2:
                    pe.wait_ge(s["gelu"], FC * (e - 1))
                pe.wait_ge(d_wt, 16 * 4)
                for n in range(FC):
                    f0 = F * e + 128 * n
                    last = pe.matmul(ps[:, (2 * e + n // 2) % 4, 256 * (n % 2):256 * (n % 2) + 256], w1s[:, f0:f0 + 128], xT[:],
                                     start=True, stop=True)
                    if n % 2:
                        last.then_inc(s["up"], 1)

            def weights(e):
                if e >= 2:
                    pe.wait_ge(s["mul"], e - 1)
                pe.matmul(ps[:, 4 + e % 2, 0:B * S], ident[0:E, e:e + 1].broadcast_to([E, 128]), wT[:], start=True, stop=True)\
                    .then_inc(s["wb"], 1)

            def down(e):
                pe.wait_ge(s["mul"], e + 1)
                for n in range(FC):
                    last = pe.matmul(ps[:, 6, 0:B * S], w2s[:, FC * e + n, :], hid[e % 4][:, n, :],
                                     start=(e == 0 and n == 0), stop=False)
                last.then_inc(s["down"], 1)

            up(0)
            up(1)
            pe.wait_ge(s["wts"], 1)
            for b in range(B):
                last = pe.transpose(ps[0:E, 7, b * S:(b + 1) * S], wr[:, b, :], ident[:])
            last.then_inc(s["wTp"], 1)
            pe.wait_ge(s["wTc"], 1)
            weights(0)
            pe.wait_ge(d_w2, 16 * 4)
            for e in range(E):
                if e + 1 < E:
                    weights(e + 1)
                if e + 2 < E:
                    up(e + 2)
                down(e)
            pe.matmul(ps[:, 6, 0:B * S], b2s[:], wT[:], start=False, stop=True).then_inc(s["y"], 1)
            pe.wait_ge(s["yc"], 1)
            for b in range(B):
                last = pe.transpose(ps[:, 7, D * b:D * b + D], yT[:, b * S:(b + 1) * S], ident[:])
            last.then_inc(s["yt"], 1)


def shape_tables():
    ident = np.eye(128, dtype=np.float32)
    blocks = np.repeat(np.eye(H, dtype=np.float32), DK, axis=0)
    inv = (np.float32(1.0) / np.float32(10000.0) ** (np.arange(0, DK, 2, dtype=np.float32) / np.float32(DK)))
    freqs = np.arange(S, dtype=np.float32)[:, None] * inv[None, :].astype(np.float32)
    sin, cos = np.sin(freqs), np.cos(freqs)
    rot = np.stack([np.concatenate([cos, cos], 1), np.concatenate([-sin, sin], 1)], 1).astype(np.float32)
    pos = np.arange(S, dtype=np.float32)
    dist = np.minimum(pos[None, :] - pos[:, None], 0).astype(np.float32)
    tri = np.broadcast_to(np.tril(np.ones((E, E), np.float32), -1)[None], (128, E, E)).copy()
    quart = np.tile(np.repeat(np.eye(GH, dtype=np.float32), DK, axis=0), (NG, 1))
    sumrow = np.zeros((128, GH), np.float32)
    sumrow[32 * np.arange(GH) + DK, np.arange(GH)] = 1
    return {"ident": ident, "blocks": blocks, "rot": rot, "dist": dist, "tri": tri, "quart": quart, "sumrow": sumrow, "ones": np.full((TERM0, CTX // 2), ONES2, np.int32)}


def kernel(**inputs):
    import numpy as _np
    import concourse.bacc as _bacc
    from concourse import mybir as _mybir
    from concourse.bass_utils import run_bass_kernel_spmd as _run

    i = {k: _np.asarray(v) for k, v in inputs.items()}
    p = "L0_xattn_"
    arrays = {
        "x": i["x"],
        "ctxT": i["ctx_1024"].transpose(0, 2, 1),
        "wq": i[p + "Wq"].T, "wk": i[p + "Wk"].T, "wv": i[p + "Wv"].T, "wo": i[p + "Wo"].T,
        "bq": i[p + "bq"][:, None], "bk": i[p + "bk"][:, None], "bv": i[p + "bv"][None], "bo": i[p + "bo"][None],
        "qkvw": i["L0_attn_qkv_w"].T, "projw": i["L0_attn_proj_w"].T, "projb": i["L0_attn_proj_b"][None],
        "slopes": i["L0_attn_slopes"][None],
        "keysT": i["L0_ffn_keys"].T,
        "w1": i["L0_ffn_w1"].transpose(2, 0, 1).reshape(D, E * F),
        "b1": i["L0_ffn_b1"].reshape(E * FC, 128).T,
        "w2": i["L0_ffn_w2"].reshape(E, D, FC, 128).transpose(3, 0, 2, 1).reshape(128, E * FC, D),
        "b2": i["L0_ffn_b2"], "rwT": i["L0_ffn_rw"].T, "rb": i["L0_ffn_rb"][None],
        **shape_tables(),
    }
    nc = _bacc.Bacc("TRN2", target_bir_lowering=False, num_devices=1)
    feed, args = {}, []
    for name, a in arrays.items():
        feed["in_" + name] = _np.ascontiguousarray(a)
        args.append(nc.dram_tensor("in_" + name, a.shape, _mybir.dt.from_np(a.dtype), kind="ExternalInput").ap())
    args.append(nc.dram_tensor("out_x", (B, S, D), _mybir.dt.float32, kind="ExternalOutput").ap())
    build(nc, *args)
    return _run(nc, [feed], core_ids=[0]).results[0]["out_x"]
```

```python
import math

import numpy as np

import concourse.bass as bass
from concourse import mybir
from contextlib import ExitStack

B, S, D, H = 2, 128, 128, 16
DK = D // H
CTX = 2048
E, F, TOP = 16, 512, 4
FC = F // 128
NK = CTX // 128
PAIRS = H // 2
GH = 4
NG = H // GH
HALF = 64
M_ROWS = 3
TERM0 = 16
TERMS = [(0, 0), (0, 1), (0, 2), (1, 0), (1, 1), (2, 0)]
STACKS = [(0, 0, 2), (0, 2, PAIRS), (1, 0, PAIRS)]
K_RUNS = [(0, 3), (3, 2), (5, 1)]
SCALE = DK ** -0.5
LN_EPS = 1e-5
CLIP = 1e-12
MAX_BIAS = 8.0
ONES2 = 0x3F803F80


def build(nc, x, ctxT, wq, wk, wv, wo, bqk, bv, bo, qkvw, projw, projb, slopes,
          keysT, w1, b1, w2, b2, rwT, rb, ident_in, blocks_in, rot_in, dist_in, tri_in, quart_in, sumrow_in, sel3_in, out):
    fp32, bf16, i32 = mybir.dt.float32, mybir.dt.bfloat16, mybir.dt.int32
    ALU, ACT, AX = mybir.AluOpType, mybir.ActivationFunctionType, mybir.AxisListType

    with ExitStack() as es:
        def sb(name, shape, dt=fp32):
            return es.enter_context(nc.sbuf_tensor(name, shape, dt))

        def sem(name):
            return es.enter_context(nc.semaphore(name))

        ident = sb("ident", [128, 128])
        identb = sb("identb", [128, 128], bf16)
        blocks = sb("blocks", [128, H])
        blocksb = sb("blocksb", [128, H], bf16)
        rot = sb("rot", [128, 2, DK])
        dist = sb("dist", [128, 128])
        tri = sb("tri", [128, E, E])
        quart = sb("quart", [128, GH])
        sumrow = sb("sumrow", [128, GH])
        xs = sb("xs", [128, B, D])
        cT = sb("cT", [128, B, CTX])
        wqs, wks, wvs, wos = (sb(n, [128, 128]) for n in ("wqs", "wks", "wvs", "wos"))
        qkvs = sb("qkvs", [128, 3 * D])
        projs = sb("projs", [128, D])
        cols = sb("cols", [128, 2])
        bvB, boB, pbB, slB = (sb(n, [128, w]) for n, w in (("bvB", D), ("boB", D), ("pbB", D), ("slB", H)))
        w1s = sb("w1s", [128, E * F])
        b1s = sb("b1s", [128, E * FC])
        b2s = sb("b2s", [E, D])
        keys_s, rw_s = sb("keys_s", [128, E]), sb("rw_s", [128, E])
        rb_s = sb("rb_s", [1, E])

        kst = sb("kst", [128, B, PAIRS, CTX], bf16)
        alibi = sb("alibi", [128, H, 128])
        kr = sb("kr", [128, 2, 1024])
        kmx = sb("kmx", [128, B * H])
        vau = sb("vau", [128, B * NK, H, DK + 1])
        qst = sb("qst", [128, PAIRS, 2, B * S], bf16)
        qf = sb("qf", [128, B * S])
        qr = sb("qr", [128, B * S])
        qp = sb("qp", [128, len(TERMS), B * S], bf16)
        NE = 4
        ex = sb("ex", [128, NE, 512])
        mx2 = sb("mx2", [128, B, H, 2])
        mx = sb("mx", [128, B, H])
        ngm = sb("ngm", [128, GH])
        ngr = sb("ngr", [128, GH])
        mpad = sb("mpad", [128, 2, GH // 2, 128], bf16)
        oS = sb("oS", [128, B, 512])
        zero = sb("zero", [128, 8])
        expo = sb("expo", [128, 64])
        st = sb("st", [128, B, 6])
        mv = sb("mv", [128, B, 2])
        rstd = sb("rstd", [128, B])
        xn = sb("xn", [128, B, D])
        xT = sb("xT", [128, B * S])
        rec = sb("rec", [128, B, H])
        cn = sb("cn", [128, B, D])
        cnT = sb("cnT", [128, B * S])
        qsq = sb("qsq", [128, B * S])
        blbk = sb("blbk", [128, H])
        kmaxc = sb("kmaxc", [B * H, 1])
        kbc = sb("kbc", [B * H, 128])
        count = sb("count", [128, 1])
        fk = sb("fk", [128, 2, 128], bf16)
        fq = sb("fq", [128, 2, 2, 128], bf16)
        fv = sb("fv", [128, GH, DK + 1])
        fo = sb("fo", [128, 128])
        facc = sb("facc", [128, 128])
        sm = sb("sm", [128, B, H])
        sl8 = sb("sl8", [128, H])
        qT = sb("qT", [128, B, 128])
        neg = sb("neg", [128, 128])
        gk = sb("gk", [128, E])
        ksq2 = sb("ksq2", [128, E])
        lg = sb("lg", [128, B, E])
        lmx = sb("lmx", [128, B])
        rk = sb("rk", [128, B, E])
        wr = sb("wr", [128, B, E])
        wsum = sb("wsum", [128, B])
        wT = sb("wT", [E, B * S])
        sel3 = sb("sel3", [3 * E, E])
        sel3b = sb("sel3b", [3 * E, E], bf16)
        wr3 = sb("wr3", [128, B, 3, E], bf16)
        wrr = sb("wrr", [128, B, E])
        w3T = sb("w3T", [3 * E, B * S], bf16)
        nrm = sb("nrm", [128, B, H])
        qbk = sb("qbk", [128, B, H])
        sumq = sb("sumq", [128, B, H])
        low = sb("low", [128, B, H])
        bad = sb("bad", [128, 1])
        onec = sb("onec", [128, 128])
        flag = sb("flag", [1, 1], i32)

        parts_d = nc.dram_tensor("parts_d", [B, 2, 3, DK * PAIRS, CTX], bf16).ap()
        qparts_d = nc.dram_tensor("qparts_d", [2, len(TERMS), DK * PAIRS, B * S], bf16).ap()

        kflat = kst[:].rearrange("p b r k -> p (b r k)").bitcast(fp32)
        w2s = kflat[:, 0:E * FC * D].rearrange("p (n d) -> p n d", d=D)
        sc = [kflat[:, 10240 + 2048 * i:12288 + 2048 * i].rearrange("p (h k) -> p h k", h=H) for i in range(B)]
        pT = [cT[:, b, :].rearrange("p (h k) -> p h k", h=H) for b in range(B)]
        cflat = cT[:].rearrange("p b k -> p (b k)")
        rope = [kflat[:, 8192 + 512 * n:8704 + 512 * n].rearrange("p (b n) -> p b n", b=B) for n in range(3)]
        rankw = [kflat[:, 10240 + 512 * n:10752 + 512 * n].rearrange("p (b e f) -> p b e f", b=B, e=E) for n in range(2)]
        kq = ex[:, 0:B, :].rearrange("p b (h k) -> p b h k", h=GH)
        xsq = qsq
        yT = kflat[:, 12288:12544]
        fe, fC = kr[:, 0, 0:512], kr[:, 0, 512:1024]
        kp = w1s[:, 0:6144].bitcast(bf16).rearrange("p (n t k) -> p n t k", n=2 * B, t=3)
        ksq = ex[:].rearrange("p n k -> p (n k)").bitcast(bf16).rearrange("p (n k) -> p n k", n=2 * NG)
        hid = [cflat[:, 1024 * i:1024 * (i + 1)].rearrange("p (f t) -> p f t", f=FC) for i in range(4)]

        ps = es.enter_context(nc.psum_tensor("ps", [128, 8, 512], fp32))

        d_x, d_w, d_wq, d_wv, d_q, d_wt, d_w2, d_out, d_const, d_bl, d_bv = (sem("d_" + n) for n in (
            "x", "w", "wq", "wv", "q", "wt", "w2", "out", "const", "bl", "bv"))
        d_c = [sem(f"d_c{n}") for n in range(2 * B)]
        d_kb = [sem(f"d_kb{n}") for n in range(len(STACKS))]
        d_kd = [sem(f"d_kd{n}") for n in range(2 * B)]
        d_qd = sem("d_qd")
        d_fg, d_fc, d_fs = sem("d_fg"), sem("d_fc"), sem("d_fs")
        s = {n: sem("s_" + n) for n in (
            "dve", "pool", "act", "pe", "init", "rstd", "xn", "xT", "xTc", "q", "qf", "qparts", "kproj", "k0", "kcast", "kr", "kparts",
            "ksq", "kn", "kmx", "v", "vau", "unitA", "redA", "mpad", "mT", "mrow", "scB", "exp", "pv",
            "blk", "kmxT", "ones", "v2", "zb", "va", "selb", "wp3", "w3c", "xe", "nrm", "redn", "lowa", "okc", "tab", "alibi", "qkv", "rope", "qkT", "qkTc", "s2", "sc2", "ex2", "pT", "pTd", "pTa",
            "pv2", "cn2", "gprep", "lgt", "lgs", "rex", "wts", "wTp", "wTc", "up", "gelu", "wb", "mul", "down", "y", "yc", "yt",
            "f_C", "f_Cc", "f_sc", "f_ex", "f_max", "f_pv", "f_add", "f_end", "f_clr",
            "oS", "oT", "bnd", "low", "cnt", "flag", "cn", "cnT", "cnTc", "o", "x1")}

        block = es.enter_context(nc.Block())

        def units():
            return [(8 * g + GH * f + j, g // NG, GH * (g % NG) + j, f)
                    for g in range(B * NG) for f in range(2) for j in range(GH)]

        UNITS = units()

        def turn_bank(g):
            return 7 if g <= NG else 6

        N_CONST = 17
        LEAD = 2
        AHEAD = 4
        LAG = 2

        kst_v = kst[:].rearrange("p b r k -> p (b r) k")
        vau_v = vau[:].rearrange("p c h d -> p (c h) d")
        oS_v = oS[:].rearrange("p b n -> p (b n)")

        def bad_rows(eng):
            eng.wait_ge(s["flag"], 1)
            return eng.value_load(flag[0:1, 0:1], min_val=0, max_val=128)

        def clip_moves(sp):
            with sp.If(bad_rows(sp)):
                with sp.Fori(0, B) as b:
                    with sp.Fori(0, NG) as n:
                        g = b * NG + n
                        for r in range(2):
                            sp.dma_start(fq[:, r], qst[:, bass.ds(2 * n + r, 1), :, bass.ds(b * S, S)]
                                         .rearrange("p r a n -> p (r a) n")).then_inc(d_fg, 16)
                        sp.dma_start(fo[:], oS_v[:, bass.ds(128 * g, 128)]).then_inc(d_fg, 16)
                        with sp.Fori(0, NK) as c:
                            it = g * NK + c
                            sp.wait_ge(s["f_pv"], it + 1)
                            sp.dma_start(fk[:], kst_v[:, bass.ds(2 * g, 2), bass.ds(128 * c, 128)]).then_inc(d_fc, 16)
                            sp.dma_start(fv[:], vau_v[:, bass.ds((b * NK + c) * H + n * GH, GH), :]).then_inc(d_fc, 16)
                        sp.wait_ge(s["f_add"], (g + 1) * NK)
                        sp.dma_start(oS_v[:, bass.ds(128 * g, 128)], facc[:]).then_inc(d_fs, 16)
                sp.wait_ge(d_fs, B * NG * 16)
                sp.wait_ge(s["f_end"], 1)

        @block.sync
        def _(sp):
            sp.dma_start(wks[:], wk).then_inc(d_w, 16)
            sp.dma_start(cT[:, 0, 0:1024], ctxT[0, :, 0:1024]).then_inc(d_c[0], 16)
            sp.dma_start(xs[:], x.rearrange("b s d -> s b d")).then_inc(d_x, 16)
            sp.dma_start(cols[:, 0:2], bqk).then_inc(d_w, 16)
            sp.dma_start(ident[:], ident_in).then_inc(d_x, 16)
            sp.dma_start(wqs[:], wq).then_inc(d_wq, 16)
            sp.dma_start(cT[:, 0, 1024:CTX], ctxT[0, :, 1024:CTX]).then_inc(d_c[1], 16)
            sp.dma_start(cT[:, 1, 0:1024], ctxT[1, :, 0:1024]).then_inc(d_c[2], 16)
            sp.dma_start(wvs[:], wv).then_inc(d_wv, 16)
            sp.dma_start(cT[:, 1, 1024:CTX], ctxT[1, :, 1024:CTX]).then_inc(d_c[3], 16)

            def parts_out(n):
                b, k0 = n // 2, 1024 * (n % 2)
                sp.wait_ge(s["kparts"], n + 1)
                for a in range(2):
                    sp.dma_start(parts_d[b, a, :, :, k0:k0 + 1024].rearrange("t r n -> r t n"), kp[HALF * a:HALF * a + HALF, n])\
                        .then_inc(d_kd[n], 16)

            def stack(i):
                b, p0, p1 = STACKS[i]
                sp.wait_ge(s["ones"], 2 * (b + 1))
                sp.wait_ge(d_kd[2 * b], 32)
                sp.wait_ge(d_kd[2 * b + 1], 32)
                for a in range(2):
                    for t0, m in K_RUNS:
                        r0 = HALF * a + TERM0 + DK * t0
                        src = parts_d[b, a, 0:m].rearrange("t (d p) n -> (t d) p n", d=DK)
                        sp.dma_start(kst[r0:r0 + DK * m, b, p0:p1, :], src[:, p0:p1, :]).then_inc(d_kb[i], 16)

            parts_out(0)
            sp.wait_ge(s["qparts"], 1)
            for a in range(2):
                sp.dma_start(qparts_d[a].rearrange("t r n -> r t n"), qp[HALF * a:HALF * a + HALF]).then_inc(d_qd, 16)
            parts_out(1)
            sp.wait_ge(s["init"], 1)
            sp.wait_ge(d_qd, 32)
            for a in range(2):
                r0 = HALF * a + TERM0
                sp.dma_start(qst[r0:HALF * a + HALF, :, a, :],
                             qparts_d[a].rearrange("t (d p) n -> (t d) p n", d=DK)).then_inc(d_q, 16)
            stack(0)
            stack(1)
            parts_out(2)
            parts_out(3)
            stack(2)
            for n in range(2 * B):
                sp.wait_ge(d_kd[n], 32)
            for n in range(4):
                sp.dma_start(w1s[:, n * E * F // 4:(n + 1) * E * F // 4], w1[:, n * E * F // 4:(n + 1) * E * F // 4])\
                    .then_inc(d_wt, 16)
            clip_moves(sp)
            sp.wait_ge(s["scB"], B * NG * NK)
            for n in range(4):
                sp.dma_start(w2s[:, 16 * n:16 * n + 16, :], w2[:, 16 * n:16 * n + 16, :]).then_inc(d_w2, 16)
            sp.wait_ge(s["x1"], 1)
            sp.dma_start(out.rearrange("b s d -> s b d"), xs[:]).then_inc(d_out, 16)
            sp.wait_ge(d_out, 16)

        @block.gpsimd
        def _(pool):
            chain = [0]

            def link(ins):
                chain[0] += 1
                ins.then_inc(s["pool"], 1)
                pool.wait_ge(s["pool"], chain[0])

            def rstds(n):
                pool.wait_ge(s["rstd"], 2 * n + 1)
                pool.tensor_tensor(rstd[:], rstd[:], expo[:, 0:B], ALU.pow).then_inc(s["rstd"], 1)

            pool.dma_start(blocks[:], blocks_in).then_inc(d_bl, 16)
            pool.dma_start(bvB[:], bv.broadcast_to([128, D])).then_inc(d_bv, 16)
            def ones(n):
                pool.memset(kst[:, n // 2, :, 1024 * (n % 2):1024 * (n % 2) + 1024].bitcast(i32), ONES2).then_inc(s["ones"], 1)

            link(pool.memset(expo[:, 0:B], -0.5))
            link(pool.memset(expo[:, 32:64], 0.5))
            ones(0)
            rstds(0)
            for n in range(1, 2 * B):
                ones(n)
            link(pool.memset(onec[:], 1.0))
            link(pool.memset(mpad[:].bitcast(i32), 0))
            link(pool.memset(vau[:, :, :, DK:DK + 1], 1.0))
            pool.sem_inc(s["init"], 1)

            for n in range(B * NK // 4):
                if n == 0:
                    pool.wait_ge(d_bv, 16)
                pool.wait_ge(s["va"], n + 1)
                v4 = vau[:, 4 * n:4 * n + 4, :, 0:DK]
                pool.tensor_tensor(v4, v4, bvB[:].rearrange("p (h d) -> p h d", h=H).unsqueeze(1).broadcast_to([128, 4, H, DK]),
                                   ALU.add).then_inc(s["vau"], 1)
            pool.wait_ge(s["nrm"], 1)
            n32 = nrm[:].rearrange("p b h -> p (b h)")
            pool.tensor_tensor(n32, n32, expo[:, 32:64], ALU.pow).then_inc(s["nrm"], 1)
            for dst, src in ((wos[:], wo), (boB[:], bo.broadcast_to([128, D])), (qkvs[:], qkvw), (projs[:], projw),
                             (pbB[:], projb.broadcast_to([128, D])), (slB[:], slopes.broadcast_to([128, H])),
                             (rot[:], rot_in), (dist[:], dist_in), (tri[:], tri_in), (quart[:], quart_in), (sumrow[:], sumrow_in),
                             (b1s[:], b1), (b2s[:], b2), (keys_s[:], keysT), (rw_s[:], rwT), (rb_s[:], rb), (sel3[:], sel3_in)):
                pool.dma_start(dst, src).then_inc(d_const, 16)
            pool.wait_ge(d_const, 16 * N_CONST)
            link(pool.tensor_scalar(sl8[:], slB[:], MAX_BIAS, None, ALU.mult))
            link(pool.tensor_tensor(alibi[:], dist[:].unsqueeze(1).broadcast_to([128, H, 128]),
                                    sl8[:].unsqueeze(2).broadcast_to([128, H, 128]), ALU.mult))
            link(pool.memset(neg[:], -1.0))
            link(pool.tensor_scalar(gk[:], keys_s[:], 2.0, None, ALU.mult))
            link(pool.tensor_tensor(gk[:], gk[:], rw_s[:], ALU.add))
            link(pool.tensor_tensor(ksq2[:], keys_s[:], keys_s[:], ALU.mult))
            pool.sem_inc(s["tab"], 1)
            rstds(1)
            rstds(2)

        @block.vector
        def _(dve):
            chain = [0]

            def link(ins):
                chain[0] += 1
                ins.then_inc(s["dve"], 1)
                dve.wait_ge(s["dve"], chain[0])

            def layer_norm(n):
                for b in range(B):
                    last = dve.bn_stats(st[:, b, :], xs[:, b, :])
                link(last)
                for b in range(B):
                    last = dve.bn_aggr(mv[:, b, :], st[:, b, :])
                link(last)
                dve.tensor_scalar(rstd[:], mv[:, :, 1], LN_EPS, None, ALU.add).then_inc(s["rstd"], 1)
                dve.wait_ge(s["rstd"], 2 * n + 2)
                for b in range(B):
                    last = dve.tensor_scalar(xn[:, b, :], xs[:, b, :], mv[:, b, 0:1], rstd[:, b:b + 1],
                                             ALU.subtract, ALU.mult)
                last.then_inc(s["xn"], 1)
                dve.wait_ge(s["xT"], n + 1)
                dve.tensor_copy(xT[:], ps[:, 7, 0:B * S]).then_inc(s["xTc"], 1)

            dve.memset(qst[:].bitcast(i32), 0).then_inc(s["init"], 1)
            dve.wait_ge(d_x, 32)
            link(dve.tensor_copy(identb[:], ident[:]))
            layer_norm(0)

            def k_parts(n):
                k3 = [kp[:, n, t, :] for t in range(3)]
                rest = kr[:, n % 2]
                dve.wait_ge(s["k0"], 2 * (n + 1))
                if n == 0:
                    dve.wait_ge(d_w, 16 * 2)
                if n >= 2:
                    dve.wait_ge(s["kparts"], n - 1)
                dve.scalar_tensor_tensor(out=rest, in0=ps[:, 2 * (n % 2):2 * (n % 2) + 2, :].rearrange("p a k -> p (a k)"),
                                         scalar=cols[:, 1:2], in1=k3[0], op0=ALU.add, op1=ALU.subtract).then_inc(s["kr"], 1)
                dve.wait_ge(s["kr"], n + 1)
                link(dve.tensor_copy(k3[1], rest))
                dve.tensor_tensor(k3[2], rest, k3[1], ALU.subtract).then_inc(s["kparts"], 1)

            k_parts(0)
            dve.wait_ge(s["qf"], 2)
            link(dve.tensor_tensor(qr[:], qf[:], qp[:, 0, :], ALU.subtract))
            link(dve.tensor_copy(qp[:, 3:5, :], qr[:].unsqueeze(1).broadcast_to([128, 2, B * S])))
            dve.tensor_tensor(qp[:, 5, :], qr[:], qp[:, 3, :], ALU.subtract).then_inc(s["qparts"], 1)
            dve.wait_ge(d_bl, 16)
            dve.tensor_copy(blocksb[:], blocks[:]).then_inc(s["blk"], 1)
            for n in range(1, 2 * B):
                k_parts(n)

            def norms_max():
                dve.wait_ge(s["kn"], 1)
                dve.tensor_reduce(out=kmx[:].rearrange("p (b h) -> p b h", b=B), in_=ps[:, 6, :].rearrange("p (b c h) -> p b h c", b=B, h=H),
                                  axis=AX.X, op=ALU.max).then_inc(s["kmx"], 1)
                dve.wait_ge(s["kmx"], 1)
                dve.memset(ps[:, 6, :], 0.0).then_inc(s["zb"], 1)
                dve.tensor_tensor(qsq[:], qf[:], qf[:], ALU.mult)
                dve.tensor_scalar(blbk[:], blocks[:], cols[:, 1:2], None, ALU.mult)

            def norms_over_all():
                dve.wait_ge(s["kmxT"], 1)
                link(dve.tensor_reduce(out=kmaxc[:], in_=ps[0:B * H, 7, 0:128], axis=AX.X, op=ALU.max))
                dve.tensor_scalar(kbc[:], kmaxc[:].broadcast_to([B * H, 128]), 1.02, None, ALU.mult).then_inc(s["bnd"], 1)

            def bound_terms():
                dve.wait_ge(s["bnd"], 2)
                bnd = [ps[:, 7, 256 + B * H * t:256 + B * H * (t + 1)].rearrange("p (b h) -> p b h", b=B) for t in range(3)]
                link(dve.tensor_copy(sumq[:], bnd[0]))
                link(dve.tensor_copy(qbk[:], bnd[2]))
                dve.tensor_tensor(nrm[:], sumq[:], bnd[1], ALU.mult).then_inc(s["nrm"], 1)
                dve.wait_ge(s["nrm"], 1)
                dve.memset(ps[:, 7, :], 0.0).then_inc(s["zb"], 1)

            def maxima(n):
                u, b, h, f = UNITS[n]
                dve.wait_ge(s["unitA"], u + 1)
                dve.tensor_reduce(out=mx2[:, b, h, f:f + 1],
                                  in_=ps[:, 2 * (u % 2):2 * (u % 2) + 2, :].rearrange("p a k -> p (a k)"),
                                  axis=AX.X, op=ALU.max).then_inc(s["redA"], 1)
                if u % 8 == 7:
                    g = u // 8
                    hs = slice(GH * (g % NG), GH * (g % NG) + GH)
                    dve.wait_ge(s["redA"], u + 1)
                    link(dve.tensor_tensor(mx[:, b, hs], mx2[:, b, hs, 0], mx2[:, b, hs, 1], ALU.max))
                    link(dve.tensor_scalar(ngm[:], mx[:, b, hs], -1.0, None, ALU.mult))
                    if g == 0:
                        dve.wait_ge(s["init"], 2)
                    m = mpad[:, g % 2].rearrange("p r (a c) -> p (r a) c", a=2)
                    link(dve.tensor_copy(m[:, :, 0], ngm[:]))
                    link(dve.tensor_tensor(ngr[:], ngm[:], m[:, :, 0], ALU.subtract))
                    link(dve.tensor_copy(m[:, :, 1], ngr[:]))
                    dve.tensor_tensor(m[:, :, 2], ngr[:], m[:, :, 1], ALU.subtract).then_inc(s["mpad"], 1)

            def rows(g):
                b, r = g // NG, 2 * (g % NG)
                dve.wait_ge(s["mT"], g + 1)
                for a in range(2):
                    last = dve.tensor_copy(
                        qst[HALF * a:HALF * a + M_ROWS, r:r + 2, a, b * S:(b + 1) * S],
                        ps[HALF * a:HALF * a + M_ROWS, turn_bank(g), 0:128].bitcast(bf16).rearrange("p (r n) -> p r n", r=2))
                last.then_inc(s["mrow"], 1)

            def normalise(b, bank, before):
                dve.wait_ge(s["oT"], before + b + 1)
                o = ps[:, bank, :].rearrange("p (n g c) -> p n g c", n=NG, g=GH)
                r4 = rec[:, b, :].rearrange("p (n g) -> p n g", n=NG)
                link(dve.reciprocal(r4, o[:, :, :, DK]))
                dve.tensor_tensor(cn[:, b, :].rearrange("p (n g d) -> p n g d", n=NG, g=GH), o[:, :, :, 0:DK],
                                  r4.unsqueeze(3).broadcast_to([128, NG, GH, DK]), ALU.mult).then_inc(s["cn"], 1)

            def sums(b):
                dve.wait_ge(s["pv"], NK * NG * (b + 1))
                dve.tensor_copy(oS[:, b, :], ps[:, 6 + b, :]).then_inc(s["oS"], 1)

            norms_max()
            norms_over_all()
            bound_terms()
            for n in range(len(UNITS)):
                maxima(n)
                if n % 8 == 0 and n:
                    rows(n // 8 - 1)
                if n == 8 * NG + 8 + LEAD - 1:
                    sums(0)
                    dve.wait_ge(d_const, 16 * N_CONST)
                    link(dve.tensor_tensor(xs[:], xs[:], boB[:].unsqueeze(1).broadcast_to([128, B, D]), ALU.add))
            rows(B * NG - 1)
            sums(B - 1)
            dve.wait_ge(s["nrm"], 2)
            link(dve.tensor_tensor(low[:], qbk[:], nrm[:], ALU.subtract))
            link(dve.tensor_tensor(low[:], low[:], mx[:], ALU.subtract))
            dve.sem_inc(s["lowa"], 1)
            for b in range(B):
                dve.wait_ge(s["oT"], b + 1)
                link(dve.tensor_copy(sumq[:, b, :].rearrange("p (n g) -> p n g", n=NG),
                                     ps[:, 4 + b, :].rearrange("p (n g c) -> p n g c", n=NG, g=GH)[:, :, :, DK]))
            dve.wait_ge(s["okc"], 1)
            link(dve.scalar_tensor_tensor(out=qbk[:], in0=sumq[:], scalar=1.01 * CLIP, in1=nrm[:], op0=ALU.mult, op1=ALU.is_le))
            dve.tensor_reduce(out=count[:], in_=qbk[:].rearrange("p b h -> p (b h)"), axis=AX.X, op=ALU.min)\
                .then_inc(s["cnt"], 1)
            dve.wait_ge(s["cnt"], 2)
            dve.tensor_scalar(flag[:], ps[0:1, 7, 0:1], -1.0, 128.0, ALU.mult, ALU.add).then_inc(s["flag"], 1)
            with dve.If(bad_rows(dve)):
                dve.memset(facc[:], 0.0).then_inc(s["f_clr"], 1)
                with dve.Fori(0, B) as b:
                    with dve.Fori(0, NG) as n:
                        g = b * NG + n
                        dve.wait_ge(s["f_C"], g + 1)
                        dve.tensor_scalar(fC, ps[:, 2, :], CLIP, None, ALU.mult).then_inc(s["f_Cc"], 1)
                        with dve.Fori(0, NK) as c:
                            it = g * NK + c
                            dve.wait_ge(s["f_Cc"], g + 1)
                            dve.wait_ge(s["f_clr"], g + 1)
                            dve.wait_ge(s["f_ex"], it + 1)
                            dve.tensor_tensor(fe, fe, fC, ALU.max).then_inc(s["f_max"], 1)
                            dve.wait_ge(s["f_pv"], it + 2)
                            for j in range(GH):
                                q = slice(32 * j, 32 * j + DK + 1)
                                last = dve.tensor_tensor(facc[q, :], facc[q, :], ps[q, 1, 0:128], ALU.add)
                            last.then_inc(s["f_add"], 1)
                            dve.wait_ge(s["f_add"], it + 1)
                        dve.wait_ge(d_fs, (g + 1) * 16)
                        dve.memset(facc[:], 0.0).then_inc(s["f_clr"], 1)
                dve.wait_ge(s["f_end"], 1)
            for b in range(B):
                normalise(b, 4 + b, 0)
            dve.wait_ge(s["cnT"], 1)
            dve.tensor_copy(cnT[:], ps[:, 7, 0:B * S]).then_inc(s["cnTc"], 1)
            dve.wait_ge(s["o"], 1)
            link(dve.tensor_tensor(xs[:], xs[:], ps[:, 6, 0:B * D].rearrange("p (b d) -> p b d", b=B), ALU.add))

            layer_norm(1)
            for b in range(B):
                dve.wait_ge(s["qkv"], b + 1)
                qk = ps[:, 4 + b, 0:2 * D].rearrange("p (h a d) -> p h a d", h=2 * H, a=2)
                t, u, r = (rope[n][:, b, :].rearrange("p (h a d) -> p h a d", h=2 * H, a=2) for n in range(3))
                cs, sn = (rot[:, n, :].rearrange("p (a d) -> p a d", a=2) for n in range(2))
                h2 = [128, 2 * H, DK // 2]
                for a in range(2):
                    dve.tensor_tensor(t[:, :, a], qk[:, :, a], cs[:, a].unsqueeze(1).broadcast_to(h2), ALU.mult)
                    last = dve.tensor_tensor(u[:, :, a], qk[:, :, 1 - a], sn[:, a].unsqueeze(1).broadcast_to(h2), ALU.mult)
                link(last)
                dve.tensor_tensor(rope[2][:, b, :], rope[0][:, b, :], rope[1][:, b, :], ALU.add).then_inc(s["rope"], 1)
            for b in range(B):
                dve.wait_ge(s["qkT"], b + 1)
                dve.tensor_copy(qT[:, b, :], ps[:, 6 + b, 0:128])
                dve.tensor_tensor(kq[:, b], ps[:, 6 + b, 128:256].unsqueeze(1).broadcast_to([128, GH, 128]),
                                  quart[:].unsqueeze(2).broadcast_to([128, GH, 128]), ALU.mult).then_inc(s["qkTc"], 1)
            dve.wait_ge(s["tab"], 1)

            def weights_back(u):
                dve.wait_ge(s["pT"], u + 1)
                dve.tensor_copy(pT[u // NG][:, 4 * (u % NG):4 * (u % NG) + 4, :],
                                ps[:, u, :].rearrange("p (h k) -> p h k", h=4)).then_inc(s["pTd"], 1)

            for u in range(B * NG):
                b, hs = u // NG, slice(GH * (u % NG), GH * (u % NG) + GH)
                dve.wait_ge(s["s2"], u + 1)
                link(dve.scalar_tensor_tensor(out=sc[b][:, hs, :].rearrange("p h k -> p (h k)"), in0=ps[:, u, :], scalar=SCALE,
                                              in1=alibi[:, hs, :].rearrange("p h k -> p (h k)"), op0=ALU.mult, op1=ALU.add))
                link(dve.tensor_reduce(out=sm[:, b, hs], in_=sc[b][:, hs, :], axis=AX.X, op=ALU.max))
                dve.tensor_scalar(sm[:, b, hs], sm[:, b, hs], -1.0, None, ALU.mult).then_inc(s["sc2"], 1)
                if u >= 2 and u % 2 == 0:
                    weights_back(u - 2)
            weights_back(B * NG - 2)
            for b in range(B):
                dve.wait_ge(s["pv2"], b + 1)
                dve.tensor_copy(oS[:, b, :], ps[:, 4 * b, :]).then_inc(s["oS"], 1)
            for b in range(B):
                normalise(b, 4 * b + 1, B)
            dve.wait_ge(s["cnT"], 2)
            dve.tensor_copy(cnT[:], ps[:, 3, 0:B * S]).then_inc(s["cnTc"], 1)
            link(dve.tensor_tensor(xs[:], xs[:], pbB[:].unsqueeze(1).broadcast_to([128, B, D]), ALU.add))
            dve.wait_ge(s["o"], 2)
            link(dve.tensor_tensor(xs[:], xs[:], ps[:, 2, 0:B * D].rearrange("p (b d) -> p b d", b=B), ALU.add))

            layer_norm(2)
            dve.wait_ge(s["xTc"], 3)
            dve.tensor_tensor(xsq[:], xT[:], xT[:], ALU.mult).then_inc(s["lgs"], 1)
            dve.wait_ge(s["lgt"], 1)
            link(dve.tensor_copy(lg[:], ps[:, 7, 256:256 + B * E].rearrange("p (b e) -> p b e", b=B)))
            link(dve.tensor_reduce(out=lmx[:], in_=lg[:], axis=AX.X, op=ALU.max))
            dve.tensor_tensor(wr[:], lg[:], lmx[:].unsqueeze(2).broadcast_to([128, B, E]), ALU.subtract).then_inc(s["rex"], 1)
            gt, eq = rankw
            for b in range(B):
                f_ = lg[:, b].unsqueeze(1).broadcast_to([128, E, E])
                e_ = lg[:, b].unsqueeze(2).broadcast_to([128, E, E])
                dve.tensor_tensor(gt[:, b], f_, e_, ALU.is_gt)
                last = dve.tensor_tensor(eq[:, b], f_, e_, ALU.is_equal)
            link(last)
            for b in range(B):
                last = dve.tensor_tensor(eq[:, b], eq[:, b], tri[:], ALU.mult)
            link(last)
            link(dve.tensor_tensor(gt.rearrange("p b e f -> p (b e f)"), gt.rearrange("p b e f -> p (b e f)"),
                                   eq.rearrange("p b e f -> p (b e f)"), ALU.add))
            link(dve.tensor_reduce(out=rk[:], in_=gt, axis=AX.X, op=ALU.add))
            dve.wait_ge(s["rex"], 2)
            link(dve.scalar_tensor_tensor(out=wr[:], in0=rk[:], scalar=TOP - 0.5, in1=wr[:], op0=ALU.is_lt, op1=ALU.mult))
            link(dve.tensor_reduce(out=wsum[:], in_=wr[:], axis=AX.X, op=ALU.add))
            link(dve.reciprocal(wsum[:], wsum[:]))
            link(dve.tensor_tensor(wr[:], wr[:], wsum[:].unsqueeze(2).broadcast_to([128, B, E]), ALU.mult))
            link(dve.tensor_copy(wr3[:, :, 0, :], wr[:]))
            link(dve.tensor_tensor(wrr[:], wr[:], wr3[:, :, 0, :], ALU.subtract))
            link(dve.tensor_copy(wr3[:, :, 1, :], wrr[:]))
            dve.tensor_tensor(wr3[:, :, 2, :], wrr[:], wr3[:, :, 1, :], ALU.subtract).then_inc(s["wts"], 1)
            dve.wait_ge(s["wTp"], 1)
            dve.tensor_copy(w3T[:], ps[0:3 * E, 5, 0:B * S // 2].bitcast(bf16)).then_inc(s["wTc"], 1)
            dve.wait_ge(s["wTp"], 2)
            dve.tensor_copy(wT[:], ps[0:E, 7, 0:B * S]).then_inc(s["wTc"], 1)
            for e in range(E):
                dve.wait_ge(s["gelu"], FC * (e + 1))
                dve.wait_ge(s["wb"], e + 1)
                dve.tensor_tensor(hid[e % AHEAD], hid[e % AHEAD],
                                  ps[:, 4 + e % 2, 0:B * S].unsqueeze(1).broadcast_to([128, FC, B * S]), ALU.mult)\
                    .then_inc(s["mul"], 1)
            dve.wait_ge(s["y"], 1)
            dve.tensor_copy(yT, ps[:, 6, 0:B * S]).then_inc(s["yc"], 1)
            dve.wait_ge(s["yt"], 1)
            dve.tensor_tensor(xs[:], xs[:], ps[:, 7, 0:B * D].rearrange("p (b d) -> p b d", b=B), ALU.add).then_inc(s["x1"], 1)

        @block.scalar
        def _(act):
            act.wait_ge(s["pool"], 1)
            act.activation(zero[:, 0:B], expo[:, 0:B], ACT.Exp)
            act.wait_ge(d_w, 16 * 2)

            def k_first(u):
                act.wait_ge(s["kproj"], u + 1)
                act.activation(kp[:, u // 2, 0, 512 * (u % 2):512 * (u % 2) + 512], ps[:, u % 4, :], ACT.Identity,
                               bias=cols[:, 1:2]).then_inc(s["k0"], 1)

            def k_square(u):
                act.wait_ge(s["kr"], u // 2 + 1)
                act.activation(ksq[:, u, :], ps[:, u % 4, :], ACT.Square).then_inc(s["ksq"], 1)

            def v_piece(n):
                act.wait_ge(s["v"], n + 1)
                act.activation(vau[:, 4 * n:4 * n + 4, :, 0:DK], ps[:, 4 + n % 2, :].rearrange("p (c h d) -> p c h d", c=4, h=H),
                               ACT.Copy).then_inc(s["va"], 1)

            k_first(0)
            k_first(1)
            k_first(2)
            act.wait_ge(s["q"], 1)
            act.activation(qf[:], ps[:, 7, 0:B * S], ACT.Identity, bias=cols[:, 0:1]).then_inc(s["qf"], 1)
            act.activation(qp[:, 0:3, :], ps[:, 7, 0:B * S].unsqueeze(1).broadcast_to([128, 3, B * S]), ACT.Identity,
                           bias=cols[:, 0:1]).then_inc(s["qf"], 1)
            k_first(3)
            k_square(0)
            k_square(1)
            v_piece(0)
            k_first(4)
            k_first(5)
            k_square(2)
            k_square(3)
            v_piece(1)
            k_first(6)
            k_first(7)
            v_piece(2)
            v_piece(3)
            for u in range(4, 8):
                k_square(u)
            for n in range(4, B * NG):
                v_piece(n)
            for g in range(B * NG):
                for c in range(NK):
                    n = NK * g + c
                    act.wait_ge(s["scB"], n + 1)
                    if n >= NE:
                        act.wait_ge(s["pv"], n - NE + 1)
                    act.activation(ex[:, n % NE, :], ps[:, 4 + n % 2, :], ACT.Exp, scale=SCALE).then_inc(s["exp"], 1)
            act.wait_ge(s["lowa"], 1)
            act.activation(nrm[:], low[:], ACT.Exp, scale=SCALE).then_inc(s["okc"], 1)
            with act.If(bad_rows(act)):
                with act.Fori(0, B * NG * NK) as it:
                    act.wait_ge(s["f_sc"], it + 1)
                    act.activation(fe, ps[:, 0, :], ACT.Exp, scale=SCALE).then_inc(s["f_ex"], 1)
            act.wait_ge(d_const, 16 * N_CONST)
            act.activation(sel3b[:], sel3[:], ACT.Copy).then_inc(s["selb"], 1)
            for b in range(B):
                act.wait_ge(s["qkv"], b + 1)
                act.wait_ge(s["rope"], b + 1)
                act.activation(vau[:, b, :, 0:DK], ps[:, 4 + b, 2 * D:3 * D].rearrange("p (h d) -> p h d", h=H), ACT.Copy)\
                    .then_inc(s["v2"], 1)

            def weights_back(u):
                act.wait_ge(s["pT"], u + 1)
                act.activation(pT[u // NG][:, 4 * (u % NG):4 * (u % NG) + 4, :], ps[:, u, :].rearrange("p (h k) -> p h k", h=4),
                               ACT.Copy).then_inc(s["pTa"], 1)

            for u in range(B * NG):
                b = u // NG
                act.wait_ge(s["sc2"], u + 1)
                for h in range(GH * (u % NG), GH * (u % NG) + GH):
                    last = act.activation(sc[b][:, h, :], sc[b][:, h, :], ACT.Exp, bias=sm[:, b, h:h + 1])
                last.then_inc(s["ex2"], 1)
                if u >= 2 and u % 2 == 0:
                    weights_back(u - 1)
            weights_back(B * NG - 1)
            act.wait_ge(s["rex"], 1)
            act.activation(wr[:], wr[:], ACT.Exp).then_inc(s["rex"], 1)
            for e in range(E):
                if e >= AHEAD:
                    act.wait_ge(s["down"], e - AHEAD + 1)
                for n in range(FC):
                    act.wait_ge(s["up"], 2 * e + n // 2 + 1)
                    act.activation(hid[e % AHEAD][:, n, :], ps[:, (2 * e + n // 2) % 4, 256 * (n % 2):256 * (n % 2) + 256], ACT.Gelu,
                                   bias=b1s[:, FC * e + n:FC * e + n + 1]).then_inc(s["gelu"], 1)

        @block.tensor
        def _(pe):
            cTf = cT[:].rearrange("p b k -> p (b k)")

            def norms(u):
                pe.wait_ge(s["ksq"], u + 1)
                if u == 0:
                    pe.wait_ge(s["blk"], 1)
                for c in range(4):
                    c0 = H * (4 * u + c)
                    last = pe.matmul(ps[:, 6, c0:c0 + H], ksq[:, u, 128 * c:128 * c + 128], blocksb[:], start=True, stop=True)
                if u == B * NG - 1:
                    last.then_inc(s["kn"], 1)

            def norms_turned():
                pe.wait_ge(s["kmx"], 1)
                pe.transpose(ps[0:B * H, 7, 0:128], kmx[:], ident[:]).then_inc(s["kmxT"], 1)

            def bound():
                pe.wait_ge(s["bnd"], 1)
                pe.matmul(ps[:, 7, 256 + B * H:256 + 2 * B * H], kbc[:], ident[0:B * H, 0:B * H], start=True, stop=True)
                for b in range(B):
                    c0 = 256 + H * b
                    pe.matmul(ps[:, 7, c0:c0 + H], qsq[:, b * S:(b + 1) * S], blocks[:], start=True, stop=True)
                    c0 += 2 * B * H
                    last = pe.matmul(ps[:, 7, c0:c0 + H], qf[:, b * S:(b + 1) * S], blbk[:], start=True, stop=True)
                last.then_inc(s["bnd"], 1)

            def keys(u):
                pe.wait_ge(d_c[u // 2], 16)
                if u >= 4:
                    pe.wait_ge(s["ksq"], u - 3)
                    pe.wait_ge(s["kr"], u // 2 - 1)
                pe.matmul(ps[:, u % 4, :], wks[:], cTf[:, 512 * u:512 * u + 512], start=True, stop=True)\
                    .then_inc(s["kproj"], 1)

            def vals(n):
                if n >= 2:
                    pe.wait_ge(s["va"], n - 1)
                pe.wait_ge(d_wv, 16)
                for j in range(4):
                    c = 4 * n + j
                    last = pe.matmul(ps[:, 4 + n % 2, 128 * j:128 * j + 128], cTf[:, 128 * c:128 * c + 128], wvs[:],
                                     start=True, stop=True)
                last.then_inc(s["v"], 1)

            pe.wait_ge(d_w, 16 * 2)
            keys(0)
            keys(1)
            pe.wait_ge(s["xn"], 1)
            for b in range(B):
                last = pe.transpose(ps[:, 7, b * S:(b + 1) * S], xn[:, b, :], ident[:])
            last.then_inc(s["xT"], 1)
            keys(2)
            pe.wait_ge(s["xTc"], 1)
            pe.wait_ge(d_wq, 16)
            pe.matmul(ps[:, 7, 0:B * S], wqs[:], xT[:], start=True, stop=True).then_inc(s["q"], 1)
            keys(3)
            vals(0)
            keys(4)
            keys(5)
            vals(1)
            keys(6)
            keys(7)
            vals(2)
            vals(3)

            def unit(n):
                u, b, h, f = UNITS[n]
                if u == 0:
                    pe.wait_ge(d_q, 32)
                    pe.wait_ge(s["ksq"], NG * B)
                    pe.wait_ge(s["kr"], 2 * B)
                for i, (bs, p0, _) in enumerate(STACKS):
                    if (bs, p0, 0, 0) == (b, h // 2, h % 2, f):
                        pe.wait_ge(d_kb[i], 32 * len(K_RUNS))
                if u >= 2:
                    pe.wait_ge(s["redA"], u - 1)
                for j in range(2):
                    k0 = 1024 * f + 512 * j
                    last = pe.matmul(ps[:, 2 * (u % 2) + j, :], qst[:, h // 2, h % 2, b * S:(b + 1) * S],
                                     kst[:, b, h // 2, k0:k0 + 512], start=True, stop=True)
                last.then_inc(s["unitA"], 1)

            def turn(g):
                pe.wait_ge(s["mpad"], g + 1)
                if g:
                    pe.wait_ge(s["mrow"], g)
                else:
                    pe.wait_ge(s["zb"], 2)
                if g == NG + 1:
                    pe.wait_ge(s["oS"], 1)
                for r in range(2):
                    last = pe.transpose(ps[:, turn_bank(g), 64 * r:64 * r + 64].bitcast(bf16), mpad[:, g % 2, r, :], identb[:])
                last.then_inc(s["mT"], 1)

            def scores(g, c):
                b, r = g // NG, 2 * (g % NG)
                n = NK * g + c
                if c == 0:
                    pe.wait_ge(s["mrow"], g + 1)
                if n == 0:
                    pe.wait_ge(s["va"], B * NK // 4)
                if n >= 2:
                    pe.wait_ge(s["exp"], n - 1)
                for j in range(2):
                    last = pe.matmul(ps[:, 4 + n % 2, 256 * j:256 * j + 256], kst[:, b, r + j, 128 * c:128 * c + 128],
                                     qst[:, r + j, :, b * S:(b + 1) * S], start=True, stop=True)
                last.then_inc(s["scB"], 1)

            def values(g, c):
                b, hg = g // NG, g % NG
                n = NK * g + c
                pe.wait_ge(s["exp"], n + 1)
                if g % NG == 0 and c % 4 == 0:
                    pe.wait_ge(s["vau"], NG * b + c // 4 + 1)
                if n == NK * NG:
                    pe.wait_ge(s["mrow"], NG + 1)
                for j in range(GH):
                    last = pe.matmul(ps[32 * j:32 * j + DK + 1, 6 + b, 128 * hg:128 * hg + 128],
                                     vau[:, NK * b + c, GH * hg + j, :], ex[:, n % NE, 128 * j:128 * j + 128],
                                     start=(c == 0), stop=(c == NK - 1), tile_position=(0, 32 * j))
                last.then_inc(s["pv"], 1)

            nu = 0

            def ahead(n):
                if n < len(UNITS):
                    unit(n)
                if n % 8 == 0 and n:
                    turn(n // 8 - 1)

            vals(4)
            vals(5)
            for u in range(B * NG):
                norms(u)
            norms_turned()
            vals(6)
            bound()
            for nu in range(8 + LEAD):
                ahead(nu)
                if nu == 1:
                    vals(7)
            nu = 8 + LEAD
            for g in range(B * NG):
                for c in range(NK):
                    scores(g, c)
                    if c % 2 == 0 and nu <= len(UNITS):
                        ahead(nu)
                        nu += 1
                    if NK * g + c >= LAG:
                        values(*divmod(NK * g + c - LAG, NK))
            for n in range(B * NG * NK - LAG, B * NG * NK):
                values(*divmod(n, NK))

            def turn_sums(b):
                for n in range(NG):
                    last = pe.transpose(ps[:, 4 + b, 128 * n:128 * n + 128], oS[:, b, 128 * n:128 * n + 128], ident[:])
                return last

            pe.wait_ge(s["exp"], B * NG * NK)
            for b in range(B):
                pe.wait_ge(s["oS"], b + 1)
                turn_sums(b).then_inc(s["oT"], 1)
            pe.wait_ge(s["cnt"], 1)
            pe.matmul(ps[0:1, 7, 0:1], count[:], onec[:, 0:1], start=True, stop=True).then_inc(s["cnt"], 1)
            with pe.If(bad_rows(pe)):
                pe.wait_ge(d_const, 16 * N_CONST)
                pe.sem_inc(s["f_pv"], 1)
                with pe.Fori(0, B * NG) as g:
                    pe.wait_ge(d_fg, (g + 1) * 48)
                    for j in range(GH):
                        last = pe.matmul(ps[:, 2, 128 * j:128 * j + 128], sumrow[:, j:j + 1].broadcast_to([128, 128]), fo[:],
                                         start=True, stop=True)
                    last.then_inc(s["f_C"], 1)
                    with pe.Fori(0, NK) as c:
                        it = g * NK + c
                        pe.wait_ge(d_fc, (it + 1) * 32)
                        for j in range(2):
                            last = pe.matmul(ps[:, 0, 256 * j:256 * j + 256], fk[:, j, :], fq[:, j].rearrange("p a n -> p (a n)"), start=True, stop=True)
                        last.then_inc(s["f_sc"], 1)
                        pe.wait_ge(s["f_max"], it + 1)
                        for j in range(GH):
                            last = pe.matmul(ps[32 * j:32 * j + DK + 1, 1, 0:128], fv[:, j, :], fe[:, 128 * j:128 * j + 128],
                                             start=True, stop=True, tile_position=(0, 32 * j))
                        last.then_inc(s["f_pv"], 1)
                        pe.wait_ge(s["f_add"], it + 1)
                pe.wait_ge(d_fs, B * NG * 16)
                turn_sums(0)
                turn_sums(1).then_inc(s["f_end"], 1)
            pe.wait_ge(s["cn"], B)
            for b in range(B):
                last = pe.transpose(ps[:, 7, b * S:(b + 1) * S], cn[:, b, :], ident[:])
            last.then_inc(s["cnT"], 1)
            pe.wait_ge(s["cnTc"], 1)
            pe.wait_ge(d_const, 16 * N_CONST)
            for b in range(B):
                last = pe.matmul(ps[:, 6, D * b:D * b + D], cnT[:, b * S:(b + 1) * S], wos[:], start=True, stop=True)
            last.then_inc(s["o"], 1)

            def turn_norm(n):
                pe.wait_ge(s["xn"], n + 1)
                for b in range(B):
                    last = pe.transpose(ps[:, 7, b * S:(b + 1) * S], xn[:, b, :], ident[:])
                last.then_inc(s["xT"], 1)
                pe.wait_ge(s["xTc"], n + 1)

            turn_norm(1)
            for b in range(B):
                pe.matmul(ps[:, 4 + b, 0:3 * D], xT[:, b * S:(b + 1) * S], qkvs[:], start=True, stop=True).then_inc(s["qkv"], 1)
            for b in range(B):
                pe.wait_ge(s["rope"], b + 1)
                for a in range(2):
                    last = pe.transpose(ps[:, 6 + b, 128 * a:128 * a + 128], rope[2][:, b, 128 * a:128 * a + 128], ident[:])
                last.then_inc(s["qkT"], 1)

            def scores2(u):
                b, n = u // NG, u % NG
                r = slice(32 * n, 32 * n + 32)
                if n == 0:
                    pe.wait_ge(s["qkTc"], B if b else 1)
                if u == NG:
                    pe.wait_ge(s["v2"], B)
                pe.matmul(ps[:, u, :], qT[r, b, :], kq[r, b].rearrange("p h k -> p (h k)"),
                          start=True, stop=True, tile_position=(32 * n, 0)).then_inc(s["s2"], 1)

            def attend(u):
                b, n = u // NG, u % NG
                if u % 2:
                    pe.wait_ge(s["pTa"], u // 2 + 1)
                else:
                    pe.wait_ge(s["pTd"], u // 2 + 1)
                if u == 0:
                    pe.wait_ge(s["v2"], B)
                for j in range(GH):
                    last = pe.matmul(ps[32 * j:32 * j + DK + 1, 4 * b, 128 * n:128 * n + 128], vau[:, b, GH * n + j, :],
                                     pT[b][:, GH * n + j, :], start=True, stop=True, tile_position=(0, 32 * j))
                if n == NG - 1:
                    last.then_inc(s["pv2"], 1)

            def turn_sums2(b):
                pe.wait_ge(s["oS"], B + b + 1)
                for n in range(NG):
                    last = pe.transpose(ps[:, 4 * b + 1, 128 * n:128 * n + 128], oS[:, b, 128 * n:128 * n + 128], ident[:])
                last.then_inc(s["oT"], 1)

            for u in range(3):
                scores2(u)
            for u in range(B * NG):
                if u + 3 < B * NG:
                    scores2(u + 3)
                pe.wait_ge(s["ex2"], u + 1)
                for j in range(GH):
                    last = pe.transpose(ps[:, u, 128 * j:128 * j + 128], sc[u // NG][:, GH * (u % NG) + j, :], ident[:])
                last.then_inc(s["pT"], 1)
                if u >= 2:
                    attend(u - 2)
            attend(B * NG - 2)
            attend(B * NG - 1)
            turn_sums2(0)
            turn_sums2(1)
            pe.wait_ge(s["cn"], 2 * B)
            for b in range(B):
                last = pe.transpose(ps[:, 3, b * S:(b + 1) * S], cn[:, b, :], ident[:])
            last.then_inc(s["cnT"], 1)
            pe.wait_ge(s["cnTc"], 2)
            for b in range(B):
                last = pe.matmul(ps[:, 2, D * b:D * b + D], cnT[:, b * S:(b + 1) * S], projs[:], start=True, stop=True)
            last.then_inc(s["o"], 1)

            turn_norm(2)
            pe.wait_ge(s["tab"], 1)
            pe.wait_ge(s["selb"], 1)
            def up(e):
                if e >= 2:
                    pe.wait_ge(s["gelu"], FC * (e - 1))
                pe.wait_ge(d_wt, 16 * 4)
                for n in range(FC):
                    f0 = F * e + 128 * n
                    last = pe.matmul(ps[:, (2 * e + n // 2) % 4, 256 * (n % 2):256 * (n % 2) + 256], w1s[:, f0:f0 + 128], xT[:],
                                     start=True, stop=True)
                    if n % 2:
                        last.then_inc(s["up"], 1)

            def weights(e):
                if e >= 2:
                    pe.wait_ge(s["mul"], e - 1)
                if e == 1:
                    pe.wait_ge(s["wTc"], 2)
                pe.matmul(ps[:, 4 + e % 2, 0:B * S], sel3b[:, e:e + 1].broadcast_to([3 * E, 128]), w3T[:], start=True, stop=True)\
                    .then_inc(s["wb"], 1)

            def down(e):
                pe.wait_ge(s["mul"], e + 1)
                for n in range(FC):
                    last = pe.matmul(ps[:, 6, 0:B * S], w2s[:, FC * e + n, :], hid[e % AHEAD][:, n, :],
                                     start=(e == 0 and n == 0), stop=False)
                last.then_inc(s["down"], 1)

            pe.wait_ge(s["lgs"], 1)
            for b in range(B):
                o = ps[:, 7, 256 + E * b:256 + E * (b + 1)]
                pe.matmul(o, xsq[:, b * S:(b + 1) * S], neg[:, 0:E], start=True, stop=False)
                pe.matmul(o, neg[:], ksq2[:], start=False, stop=False)
                pe.matmul(o, xT[:, b * S:(b + 1) * S], gk[:], start=False, stop=False)
                last = pe.matmul(o, onec[0:1, :], rb_s[:], start=False, stop=True)
            last.then_inc(s["lgt"], 1)
            for e in range(AHEAD):
                up(e)
            pe.wait_ge(s["wts"], 1)
            for b in range(B):
                last = pe.transpose(ps[0:3 * E, 5, b * S // 2:(b + 1) * S // 2].bitcast(bf16),
                                    wr3[:, b].rearrange("p t e -> p (t e)"), identb[:])
            last.then_inc(s["wTp"], 1)
            for b in range(B):
                last = pe.transpose(ps[0:E, 7, b * S:(b + 1) * S], wr[:, b, :], ident[:])
            last.then_inc(s["wTp"], 1)
            pe.wait_ge(s["wTc"], 1)
            weights(0)
            pe.wait_ge(d_w2, 16 * 4)
            for e in range(E):
                if e + 1 < E:
                    weights(e + 1)
                down(e)
                if e + AHEAD < E:
                    up(e + AHEAD)
            pe.matmul(ps[:, 6, 0:B * S], b2s[:], wT[:], start=False, stop=True).then_inc(s["y"], 1)
            pe.wait_ge(s["yc"], 1)
            for b in range(B):
                last = pe.transpose(ps[:, 7, D * b:D * b + D], yT[:, b * S:(b + 1) * S], ident[:])
            last.then_inc(s["yt"], 1)


ROWS = np.arange(D).reshape(PAIRS, 2, DK).transpose(1, 2, 0).reshape(D)


def shape_tables():
    ident = np.eye(128, dtype=np.float32)
    blocks = np.eye(H, dtype=np.float32)[ROWS // DK]
    inv = (np.float32(1.0) / np.float32(10000.0) ** (np.arange(0, DK, 2, dtype=np.float32) / np.float32(DK)))
    freqs = np.arange(S, dtype=np.float32)[:, None] * inv[None, :].astype(np.float32)
    sin, cos = np.sin(freqs), np.cos(freqs)
    rot = np.stack([np.concatenate([cos, cos], 1), np.concatenate([-sin, sin], 1)], 1).astype(np.float32)
    pos = np.arange(S, dtype=np.float32)
    dist = np.minimum(pos[None, :] - pos[:, None], 0).astype(np.float32)
    tri = np.broadcast_to(np.tril(np.ones((E, E), np.float32), -1)[None], (128, E, E)).copy()
    quart = np.tile(np.repeat(np.eye(GH, dtype=np.float32), DK, axis=0), (NG, 1))
    sumrow = np.zeros((128, GH), np.float32)
    sumrow[32 * np.arange(GH) + DK, np.arange(GH)] = 1
    return {"ident": ident, "blocks": blocks, "rot": rot, "dist": dist, "tri": tri, "quart": quart, "sumrow": sumrow, "sel3": np.tile(np.eye(E, dtype=np.float32), (3, 1)),}


def kernel(**inputs):
    import numpy as _np
    import concourse.bacc as _bacc
    from concourse import mybir as _mybir
    from concourse.bass_utils import run_bass_kernel_spmd as _run

    i = {k: _np.asarray(v) for k, v in inputs.items()}
    p = "L0_xattn_"
    arrays = {
        "x": i["x"],
        "ctxT": i["ctx_1024"].transpose(0, 2, 1),
        "wq": i[p + "Wq"][ROWS].T, "wk": i[p + "Wk"][ROWS].T, "wv": i[p + "Wv"].T, "wo": i[p + "Wo"].T,
        "bqk": _np.stack([i[p + "bq"][ROWS], i[p + "bk"][ROWS]], axis=1), "bv": i[p + "bv"][None], "bo": i[p + "bo"][None],
        "qkvw": i["L0_attn_qkv_w"].T, "projw": i["L0_attn_proj_w"].T, "projb": i["L0_attn_proj_b"][None],
        "slopes": i["L0_attn_slopes"][None],
        "keysT": i["L0_ffn_keys"].T,
        "w1": i["L0_ffn_w1"].transpose(2, 0, 1).reshape(D, E * F),
        "b1": i["L0_ffn_b1"].reshape(E * FC, 128).T,
        "w2": i["L0_ffn_w2"].reshape(E, D, FC, 128).transpose(3, 0, 2, 1).reshape(128, E * FC, D),
        "b2": i["L0_ffn_b2"], "rwT": i["L0_ffn_rw"].T, "rb": i["L0_ffn_rb"][None],
        **shape_tables(),
    }
    nc = _bacc.Bacc("TRN2", target_bir_lowering=False, num_devices=1)
    feed, args = {}, []
    for name, a in arrays.items():
        feed["in_" + name] = _np.ascontiguousarray(a)
        args.append(nc.dram_tensor("in_" + name, a.shape, _mybir.dt.from_np(a.dtype), kind="ExternalInput").ap())
    args.append(nc.dram_tensor("out_x", (B, S, D), _mybir.dt.float32, kind="ExternalOutput").ap())
    build(nc, *args)
    return _run(nc, [feed], core_ids=[0]).results[0]["out_x"]
```

```python
import numpy as np

import concourse.bass as bass
from concourse import mybir
from contextlib import ExitStack

B, S, D, H = 2, 128, 128, 16
DK = D // H
CTX = 2048
E, F, TOP = 16, 512, 4
FC = F // 128
NK = CTX // 128
PAIRS = H // 2
GH = 4
NG = H // GH
HALF = 64
M_ROWS = 3
TERM0 = 16
TERMS = [(0, 0), (0, 1), (0, 2), (1, 0), (1, 1), (2, 0)]
STACKS = [(0, 0, 2), (0, 2, PAIRS), (1, 0, PAIRS)]
K_RUNS = [(0, 3), (3, 2), (5, 1)]
SCALE = DK ** -0.5
LN_EPS = 1e-5
CLIP = 1e-12
MAX_BIAS = 8.0
MINUS_ONES2 = 0xBF80BF80 - (1 << 32)


def build(nc, x, ctxT, wq, wk, wv, wo, bqk, bv, bo, qkvw, projw, projb, slopes,
          keysT, w1, b1, w2, b2, rwT, rb, ident_in, blocks_in, rot_in, dist_in, tri_in, quart_in, sumrow_in, sel3_in, out):
    fp32, bf16, i32 = mybir.dt.float32, mybir.dt.bfloat16, mybir.dt.int32
    ALU, ACT, AX = mybir.AluOpType, mybir.ActivationFunctionType, mybir.AxisListType

    with ExitStack() as es:
        def sb(name, shape, dt=fp32):
            return es.enter_context(nc.sbuf_tensor(name, shape, dt))

        def sem(name):
            return es.enter_context(nc.semaphore(name))

        ident = sb("ident", [128, 128])
        identb = sb("identb", [128, 128], bf16)
        blocks = sb("blocks", [128, H])
        blocksb = sb("blocksb", [128, H], bf16)
        rot = sb("rot", [128, 2, DK])
        dist = sb("dist", [128, 128])
        tri = sb("tri", [128, E, E])
        quart = sb("quart", [128, GH])
        sumrow = sb("sumrow", [128, GH])
        xs = sb("xs", [128, B, D])
        cT = sb("cT", [128, B, CTX])
        wqs, wks, wvs, wos = (sb(n, [128, 128]) for n in ("wqs", "wks", "wvs", "wos"))
        qkvs = sb("qkvs", [128, 3 * D])
        projs = sb("projs", [128, D])
        cols = sb("cols", [128, 2])
        bvB, boB, pbB, slB = (sb(n, [128, w]) for n, w in (("bvB", D), ("boB", D), ("pbB", D), ("slB", H)))
        w1s = sb("w1s", [128, E * F])
        b1s = sb("b1s", [128, E * FC])
        b2s = sb("b2s", [E, D])
        keys_s, rw_s = sb("keys_s", [128, E]), sb("rw_s", [128, E])
        rb_s = sb("rb_s", [1, E])

        kst = sb("kst", [128, B, PAIRS, CTX], bf16)
        alibi = sb("alibi", [128, H, 128])
        kr = sb("kr", [128, 2, 1024])
        kmx = sb("kmx", [128, B * H])
        vau = sb("vau", [128, B * NK, H, DK + 1])
        qst = sb("qst", [128, PAIRS, 2, B * S], bf16)
        qf = sb("qf", [128, B * S])
        qr = sb("qr", [128, B * S])
        qp = sb("qp", [128, len(TERMS), B * S], bf16)
        NE = 4
        ex = sb("ex", [128, NE, 512])
        mx2 = sb("mx2", [128, B, H, 2])
        mx = sb("mx", [128, B, H])
        mxr = sb("mxr", [128, GH])
        mpad = sb("mpad", [128, 2, GH // 2, 128], bf16)
        oS = sb("oS", [128, B, 512])
        zero = sb("zero", [128, 8])
        expo = sb("expo", [128, 64])
        st = sb("st", [128, B, 6])
        mv = sb("mv", [128, B, 2])
        rstd = sb("rstd", [128, B])
        xn = sb("xn", [128, B, D])
        xT = sb("xT", [128, B * S])
        rec = sb("rec", [128, B, H])
        cn = sb("cn", [128, B, D])
        cnT = sb("cnT", [128, B * S])
        qsq = sb("qsq", [128, B * S])
        blbk = sb("blbk", [128, H])
        kmaxc = sb("kmaxc", [B * H, 1])
        kbc = sb("kbc", [B * H, 128])
        count = sb("count", [128, B])
        fk = sb("fk", [128, 2, 128], bf16)
        fq = sb("fq", [128, 2, 2, 128], bf16)
        fv = sb("fv", [128, GH, DK + 1])
        fo = sb("fo", [128, 128])
        facc = sb("facc", [128, 128])
        sm = sb("sm", [128, B, H])
        sl8 = sb("sl8", [128, H])
        qT = sb("qT", [128, B, 128])
        kq = sb("kq", [128, B, GH, 128])
        rope0 = sb("rope0", [128, 3, 2 * D])
        neg = sb("neg", [128, 128])
        gk = sb("gk", [128, E])
        ksq2 = sb("ksq2", [128, E])
        lg = sb("lg", [128, B, E])
        lmx = sb("lmx", [128, B])
        x2s = sb("x2s", [128, B])
        rk = sb("rk", [128, B, E])
        wr = sb("wr", [128, B, E])
        wsum = sb("wsum", [128, B])
        wT = sb("wT", [E, B * S])
        sel3 = sb("sel3", [3 * E, E])
        sel3b = sb("sel3b", [3 * E, E], bf16)
        wr3 = sb("wr3", [128, B, 3, E], bf16)
        wrr = sb("wrr", [128, B, E])
        w3T = sb("w3T", [3 * E, B * S], bf16)
        nrm = sb("nrm", [128, B, H])
        qbk = sb("qbk", [128, B, H])
        sumq = sb("sumq", [128, B, H])
        low = sb("low", [128, B, H])
        onec = sb("onec", [128, 128])
        flag = sb("flag", [1, B], i32)

        parts_d = nc.dram_tensor("parts_d", [B, 2, 3, DK * PAIRS, CTX], bf16).ap()
        qparts_d = nc.dram_tensor("qparts_d", [2, len(TERMS), DK * PAIRS, B * S], bf16).ap()

        kflat = kst[:].rearrange("p b r k -> p (b r k)").bitcast(fp32)
        w2s = kflat[:, 0:E * FC * D].rearrange("p (n d) -> p n d", d=D)
        sc = [v.rearrange("p (h k) -> p h k", h=H) for v in (cT[:, 1, :], kflat[:, 12288:14336])]
        pT = [cT[:, b, :].rearrange("p (h k) -> p h k", h=H) for b in range(B)]
        cflat = cT[:].rearrange("p b k -> p (b k)")
        rope = [rope0[:], kflat[:, 8192:8192 + 6 * D].rearrange("p (t n) -> p t n", t=3)]
        rankw = [kflat[:, 10240 + 512 * n:10752 + 512 * n].rearrange("p (b e f) -> p b e f", b=B, e=E) for n in range(2)]
        yT = kflat[:, 12288:12544]
        fe, fC = kr[:, 0, 0:512], kr[:, 0, 512:1024]
        kp = w1s[:, 0:6144].bitcast(bf16).rearrange("p (n t k) -> p n t k", n=2 * B, t=3)
        ksq = ex[:].rearrange("p n k -> p (n k)").bitcast(bf16).rearrange("p (n k) -> p n k", n=2 * NG)
        hid = [cflat[:, 1024 * i:1024 * (i + 1)].rearrange("p (f t) -> p f t", f=FC) for i in range(4)]

        ps = es.enter_context(nc.psum_tensor("ps", [128, 8, 512], fp32))

        d_x, d_w, d_wq, d_wv, d_q, d_wt, d_w2, d_out, d_const, d_bl, d_bv = (sem("d_" + n) for n in (
            "x", "w", "wq", "wv", "q", "wt", "w2", "out", "const", "bl", "bv"))
        d_c0 = sem("d_c00")
        d_c = [sem(f"d_c{n}") for n in range(2 * B)]
        d_kb = [sem(f"d_kb{n}") for n in range(len(STACKS))]
        d_kd = [sem(f"d_kd{n}") for n in range(2 * B)]
        d_qd = sem("d_qd")
        d_fg, d_fc, d_fs = ([sem(f"d_{n}{b}") for b in range(B)] for n in ("fg", "fc", "fs"))
        f_C, f_Cc, f_sc, f_ex, f_max, f_pv, f_add, f_end, f_clr = ([sem(f"s_f_{n}{b}") for b in range(B)] for n in (
            "C", "Cc", "sc", "ex", "max", "pv", "add", "end", "clr"))
        s = {n: sem("s_" + n) for n in (
            "dve", "pool", "init", "rstd", "xn", "xT", "xTc", "q", "qf", "qparts", "kproj", "k0", "kr", "kparts",
            "ksq", "kn", "kmx", "v", "vau", "unitA", "redA", "mpad", "mT", "mrow", "scB", "exp", "pv", "blk", "kmxT",
            "ones", "v2", "zb", "va", "selb", "nrm", "lowa", "okc", "tab", "qkv", "rope", "qkT", "qkTc", "s2", "sc2",
            "ex2", "pT", "pTd", "pTa", "pv2", "lgt", "rex", "wts", "wTp", "wTc", "up", "gelu", "wb", "mul", "down",
            "yc", "yt", "oS", "oT", "bnd", "bndq", "cnt", "flag", "cn", "cnT", "cnTc", "o", "x1")}

        block = es.enter_context(nc.Block())

        def units():
            return [(8 * g + GH * f + j, g // NG, GH * (g % NG) + j, f)
                    for g in range(B * NG) for f in range(2) for j in range(GH)]

        UNITS = units()

        def turn_bank(g):
            return 7 if g <= NG else 6

        N_CONST = 17
        LEAD = 2
        AHEAD = 4
        TAIL = [2, 7]
        LAG = 3

        kst_v = kst[:].rearrange("p b r k -> p (b r) k")
        vau_v = vau[:].rearrange("p c h d -> p (c h) d")
        oS_v = oS[:].rearrange("p b n -> p (b n)")

        CHECK = NK * (B * NG - 1) - 4

        def bad_rows(eng, b):
            eng.wait_ge(s["flag"], b + 1)
            return eng.value_load(flag[0:1, b:b + 1], min_val=0, max_val=128)

        def clip_moves(sp, b):
            with sp.If(bad_rows(sp, b)):
                with sp.Fori(0, NG) as n:
                    for r in range(2):
                        sp.dma_start(fq[:, r], qst[:, bass.ds(2 * n + r, 1), :, b * S:(b + 1) * S]
                                     .rearrange("p r a n -> p (r a) n")).then_inc(d_fg[b], 16)
                    sp.dma_start(fo[:], oS[:, b, bass.ds(128 * n, 128)]).then_inc(d_fg[b], 16)
                    with sp.Fori(0, NK) as c:
                        it = n * NK + c
                        sp.wait_ge(f_pv[b], it + 1)
                        sp.dma_start(fk[:], kst[:, b, bass.ds(2 * n, 2), bass.ds(128 * c, 128)]).then_inc(d_fc[b], 16)
                        sp.dma_start(fv[:], vau_v[:, bass.ds(c * H + n * GH + b * NK * H, GH), :]).then_inc(d_fc[b], 16)
                    sp.wait_ge(f_add[b], (n + 1) * NK)
                    sp.dma_start(oS[:, b, bass.ds(128 * n, 128)], facc[:]).then_inc(d_fs[b], 16)
                sp.wait_ge(d_fs[b], NG * 16)
                sp.wait_ge(f_end[b], 1)

        @block.sync
        def _(sp):
            sp.dma_start(wks[:], wk).then_inc(d_w, 16)
            sp.dma_start(cT[:, 0, 0:512], ctxT[0, :, 0:512]).then_inc(d_c0, 16)
            sp.dma_start(cT[:, 0, 512:1024], ctxT[0, :, 512:1024]).then_inc(d_c[0], 16)
            sp.dma_start(xs[:], x.rearrange("b s d -> s b d")).then_inc(d_x, 16)
            sp.dma_start(cols[:, 0:2], bqk).then_inc(d_w, 16)
            sp.dma_start(ident[:], ident_in).then_inc(d_x, 16)
            sp.dma_start(wqs[:], wq).then_inc(d_wq, 16)
            sp.dma_start(cT[:, 0, 1024:CTX], ctxT[0, :, 1024:CTX]).then_inc(d_c[1], 16)
            sp.dma_start(cT[:, 1, 0:1024], ctxT[1, :, 0:1024]).then_inc(d_c[2], 16)
            sp.dma_start(wvs[:], wv).then_inc(d_wv, 16)
            sp.dma_start(cT[:, 1, 1024:CTX], ctxT[1, :, 1024:CTX]).then_inc(d_c[3], 16)

            def parts_out(n):
                b, k0 = n // 2, 1024 * (n % 2)
                sp.wait_ge(s["kparts"], n + 1)
                for a in range(2):
                    sp.dma_start(parts_d[b, a, :, :, k0:k0 + 1024].rearrange("t r n -> r t n"), kp[HALF * a:HALF * a + HALF, n])\
                        .then_inc(d_kd[n], 16)

            def stack(i, parities=(0, 1)):
                b, p0, p1 = STACKS[i]
                sp.wait_ge(s["ones"], 2 * (b + 1))
                sp.wait_ge(d_kd[2 * b], 32)
                sp.wait_ge(d_kd[2 * b + 1], 32)
                for a in parities:
                    for t0, m in K_RUNS:
                        r0 = HALF * a + TERM0 + DK * t0
                        src = parts_d[b, a, 0:m].rearrange("t (d p) n -> (t d) p n", d=DK)
                        sp.dma_start(kst[r0:r0 + DK * m, b, p0:p1, :], src[:, p0:p1, :]).then_inc(d_kb[i], 16)

            parts_out(0)
            parts_out(1)
            sp.wait_ge(s["qparts"], 1)
            for a in range(2):
                sp.dma_start(qparts_d[a].rearrange("t r n -> r t n"), qp[HALF * a:HALF * a + HALF]).then_inc(d_qd, 16)
            stack(0, [0])
            sp.wait_ge(s["init"], 1)
            sp.wait_ge(d_qd, 32)
            for a in range(2):
                r0 = HALF * a + TERM0
                sp.dma_start(qst[r0:HALF * a + HALF, :, a, :],
                             qparts_d[a].rearrange("t (d p) n -> (t d) p n", d=DK)).then_inc(d_q, 16)
            stack(0, [1])
            stack(1)
            parts_out(2)
            parts_out(3)
            stack(2)
            for n in range(2 * B):
                sp.wait_ge(d_kd[n], 32)
            for n in range(4):
                sp.dma_start(w1s[:, n * E * F // 4:(n + 1) * E * F // 4], w1[:, n * E * F // 4:(n + 1) * E * F // 4])\
                    .then_inc(d_wt, 16)
            clip_moves(sp, 0)
            sp.wait_ge(s["scB"], NG * NK)
            for n in range(4):
                sp.dma_start(w2s[:, 16 * n:16 * n + 16, :], w2[:, 16 * n:16 * n + 16, :]).then_inc(d_w2, 16)
            clip_moves(sp, 1)
            sp.wait_ge(s["x1"], 1)
            sp.dma_start(out.rearrange("b s d -> s b d"), xs[:]).then_inc(d_out, 16)
            sp.wait_ge(d_out, 16)

        @block.gpsimd
        def _(pool):
            chain = [0]

            def link(ins):
                chain[0] += 1
                ins.then_inc(s["pool"], 1)
                pool.wait_ge(s["pool"], chain[0])

            def rstds(n, b0=0, b1=B):
                pool.wait_ge(s["rstd"], 2 * n + 1)
                pool.tensor_tensor(rstd[:, b0:b1], rstd[:, b0:b1], expo[:, b0:b1], ALU.pow).then_inc(s["rstd"], 1)

            pool.dma_start(blocks[:], blocks_in).then_inc(d_bl, 16)
            pool.dma_start(bvB[:], bv.broadcast_to([128, D])).then_inc(d_bv, 16)
            def ones(n):
                pool.memset(kst[:, n // 2, :, 1024 * (n % 2):1024 * (n % 2) + 1024].bitcast(i32), MINUS_ONES2).then_inc(s["ones"], 1)

            link(pool.memset(expo[:, 0:B], -0.5))
            link(pool.memset(expo[:, 32:64], 0.5))
            ones(0)
            rstds(0)
            for n in range(1, 2 * B):
                ones(n)
            link(pool.memset(onec[:], 1.0))
            link(pool.memset(mpad[:].bitcast(i32), 0))
            link(pool.memset(vau[:, :, :, DK:DK + 1], 1.0))
            pool.sem_inc(s["init"], 1)

            for n in range(B * NK // 4):
                if n == 0:
                    pool.wait_ge(d_bv, 16)
                pool.wait_ge(s["va"], n + 1)
                v4 = vau[:, 4 * n:4 * n + 4, :, 0:DK]
                pool.tensor_tensor(v4, v4, bvB[:].rearrange("p (h d) -> p h d", h=H).unsqueeze(1).broadcast_to([128, 4, H, DK]),
                                   ALU.add).then_inc(s["vau"], 1)
            pool.wait_ge(s["nrm"], 1)
            n32 = nrm[:].rearrange("p b h -> p (b h)")
            pool.tensor_tensor(n32, n32, expo[:, 32:64], ALU.pow).then_inc(s["nrm"], 1)
            for dst, src in ((wos[:], wo), (boB[:], bo.broadcast_to([128, D])), (qkvs[:], qkvw), (projs[:], projw),
                             (pbB[:], projb.broadcast_to([128, D])), (slB[:], slopes.broadcast_to([128, H])),
                             (rot[:], rot_in), (dist[:], dist_in), (tri[:], tri_in), (quart[:], quart_in), (sumrow[:], sumrow_in),
                             (b1s[:], b1), (b2s[:], b2), (keys_s[:], keysT), (rw_s[:], rwT), (rb_s[:], rb), (sel3[:], sel3_in)):
                pool.dma_start(dst, src).then_inc(d_const, 16)
            pool.wait_ge(d_const, 16 * N_CONST)
            link(pool.tensor_scalar(sl8[:], slB[:], MAX_BIAS, None, ALU.mult))
            link(pool.tensor_tensor(alibi[:], dist[:].unsqueeze(1).broadcast_to([128, H, 128]),
                                    sl8[:].unsqueeze(2).broadcast_to([128, H, 128]), ALU.mult))
            link(pool.memset(neg[:], -1.0))
            link(pool.tensor_scalar(gk[:], keys_s[:], 2.0, None, ALU.mult))
            link(pool.tensor_tensor(gk[:], gk[:], rw_s[:], ALU.add))
            link(pool.tensor_tensor(ksq2[:], keys_s[:], keys_s[:], ALU.mult))
            link(pool.tensor_tensor(xs[:], xs[:], boB[:].unsqueeze(1).broadcast_to([128, B, D]), ALU.add))
            pool.sem_inc(s["tab"], 1)
            rstds(1, 0, 1)
            rstds(2, 1, 2)
            rstds(3, 0, 1)
            rstds(4, 1, 2)

        @block.vector
        def _(dve):
            chain = [0]

            def link(ins):
                chain[0] += 1
                ins.then_inc(s["dve"], 1)
                dve.wait_ge(s["dve"], chain[0])

            def variances(bs):
                for b in bs:
                    last = dve.bn_stats(st[:, b, :], xs[:, b, :])
                link(last)
                for b in bs:
                    last = dve.bn_aggr(mv[:, b, :], st[:, b, :])
                link(last)
                b0, b1 = bs[0], bs[-1] + 1
                dve.tensor_scalar(rstd[:, b0:b1], mv[:, b0:b1, 1], LN_EPS, None, ALU.add).then_inc(s["rstd"], 1)

            def normed(n, bs):
                dve.wait_ge(s["rstd"], 2 * n + 2)
                for b in bs:
                    last = dve.tensor_scalar(xn[:, b, :], xs[:, b, :], mv[:, b, 0:1], rstd[:, b:b + 1],
                                             ALU.subtract, ALU.mult)
                last.then_inc(s["xn"], 1)

            def normed_turned(n, bs, src):
                dve.wait_ge(s["xT"], n + 1)
                dve.tensor_copy(xT[:, bs[0] * S:(bs[-1] + 1) * S], src).then_inc(s["xTc"], 1)

            def layer_norm(n):
                bs = range(B)
                variances(bs)
                normed(n, bs)
                normed_turned(n, bs, ps[:, 7, 0:B * S])

            dve.memset(qst[:].bitcast(i32), 0).then_inc(s["init"], 1)
            dve.wait_ge(d_x, 32)
            link(dve.tensor_copy(identb[:], ident[:]))
            layer_norm(0)

            def k_parts(n):
                k3 = [kp[:, n, t, :] for t in range(3)]
                rest = kr[:, n % 2]
                dve.wait_ge(s["k0"], 2 * (n + 1))
                if n == 0:
                    dve.wait_ge(d_w, 16 * 2)
                if n >= 2:
                    dve.wait_ge(s["kparts"], n - 1)
                dve.scalar_tensor_tensor(out=rest, in0=ps[:, 2 * (n % 2):2 * (n % 2) + 2, :].rearrange("p a k -> p (a k)"),
                                         scalar=cols[:, 1:2], in1=k3[0], op0=ALU.add, op1=ALU.subtract).then_inc(s["kr"], 1)
                dve.wait_ge(s["kr"], n + 1)
                link(dve.tensor_copy(k3[1], rest))
                dve.tensor_tensor(k3[2], rest, k3[1], ALU.subtract).then_inc(s["kparts"], 1)

            k_parts(0)
            k_parts(1)
            dve.wait_ge(s["qf"], 2)
            link(dve.tensor_tensor(qr[:], qf[:], qp[:, 0, :], ALU.subtract))
            link(dve.tensor_copy(qp[:, 3:5, :], qr[:].unsqueeze(1).broadcast_to([128, 2, B * S])))
            dve.tensor_tensor(qp[:, 5, :], qr[:], qp[:, 3, :], ALU.subtract).then_inc(s["qparts"], 1)
            dve.wait_ge(d_bl, 16)
            dve.tensor_copy(blocksb[:], blocks[:]).then_inc(s["blk"], 1)
            for n in range(2, 2 * B):
                k_parts(n)

            def norms_max():
                dve.wait_ge(s["kn"], 1)
                dve.tensor_reduce(out=kmx[:].rearrange("p (b h) -> p b h", b=B), in_=ps[:, 6, :].rearrange("p (b c h) -> p b h c", b=B, h=H),
                                  axis=AX.X, op=ALU.max).then_inc(s["kmx"], 1)
                dve.wait_ge(s["kmx"], 1)
                dve.memset(ps[:, 6, :], 0.0).then_inc(s["zb"], 1)
                dve.tensor_tensor(qsq[:], qf[:], qf[:], ALU.mult)
                dve.tensor_scalar(blbk[:], blocks[:], cols[:, 1:2], None, ALU.mult).then_inc(s["bndq"], 1)

            def norms_over_all():
                dve.wait_ge(s["kmxT"], 1)
                link(dve.tensor_reduce(out=kmaxc[:], in_=ps[0:B * H, 3, 0:128], axis=AX.X, op=ALU.max))
                dve.tensor_scalar(kbc[:], kmaxc[:].broadcast_to([B * H, 128]), 1.02, None, ALU.mult).then_inc(s["bnd"], 1)

            def bound_terms():
                dve.wait_ge(s["bnd"], 2)
                bnd = [ps[:, 7, 256 + B * H * t:256 + B * H * (t + 1)].rearrange("p (b h) -> p b h", b=B) for t in range(3)]
                link(dve.tensor_copy(sumq[:], bnd[0]))
                link(dve.tensor_copy(qbk[:], bnd[2]))
                dve.tensor_tensor(nrm[:], sumq[:], bnd[1], ALU.mult).then_inc(s["nrm"], 1)
                dve.wait_ge(s["nrm"], 1)
                dve.memset(ps[:, 7, :], 0.0).then_inc(s["zb"], 1)

            def maxima(n):
                u, b, h, f = UNITS[n]
                dve.wait_ge(s["unitA"], u + 1)
                dve.tensor_reduce(out=mx2[:, b, h, f:f + 1],
                                  in_=ps[:, 2 * (u % 2):2 * (u % 2) + 2, :].rearrange("p a k -> p (a k)"),
                                  axis=AX.X, op=ALU.max).then_inc(s["redA"], 1)
                if u % 8 == 7:
                    g = u // 8
                    hs = slice(GH * (g % NG), GH * (g % NG) + GH)
                    dve.wait_ge(s["redA"], u + 1)
                    link(dve.tensor_tensor(mx[:, b, hs], mx2[:, b, hs, 0], mx2[:, b, hs, 1], ALU.max))
                    if g == 0:
                        dve.wait_ge(s["init"], 2)
                    m = mpad[:, g % 2].rearrange("p r (a c) -> p (r a) c", a=2)
                    link(dve.tensor_copy(m[:, :, 0], mx[:, b, hs]))
                    link(dve.tensor_tensor(mxr[:], mx[:, b, hs], m[:, :, 0], ALU.subtract))
                    link(dve.tensor_copy(m[:, :, 1], mxr[:]))
                    dve.tensor_tensor(m[:, :, 2], mxr[:], m[:, :, 1], ALU.subtract).then_inc(s["mpad"], 1)

            def rows(g):
                b, r = g // NG, 2 * (g % NG)
                dve.wait_ge(s["mT"], g + 1)
                for a in range(2):
                    last = dve.tensor_copy(
                        qst[HALF * a:HALF * a + M_ROWS, r:r + 2, a, b * S:(b + 1) * S],
                        ps[HALF * a:HALF * a + M_ROWS, turn_bank(g), 0:128].bitcast(bf16).rearrange("p (r n) -> p r n", r=2))
                last.then_inc(s["mrow"], 1)

            def normalise(b, bank, before):
                dve.wait_ge(s["oT"], before + b + 1)
                o = ps[:, bank, :].rearrange("p (n g c) -> p n g c", n=NG, g=GH)
                r4 = rec[:, b, :].rearrange("p (n g) -> p n g", n=NG)
                link(dve.reciprocal(r4, o[:, :, :, DK]))
                dve.tensor_tensor(cn[:, b, :].rearrange("p (n g d) -> p n g d", n=NG, g=GH), o[:, :, :, 0:DK],
                                  r4.unsqueeze(3).broadcast_to([128, NG, GH, DK]), ALU.mult).then_inc(s["cn"], 1)

            def lowest(b):
                if b == 0:
                    dve.wait_ge(s["nrm"], 2)
                link(dve.tensor_tensor(low[:, b], qbk[:, b], nrm[:, b], ALU.subtract))
                dve.tensor_tensor(low[:, b], low[:, b], mx[:, b], ALU.subtract).then_inc(s["lowa"], 1)

            def check(b):
                dve.wait_ge(s["oT"], b + 1)
                link(dve.tensor_copy(sumq[:, b, :].rearrange("p (n g) -> p n g", n=NG),
                                     ps[:, 4 * b, :].rearrange("p (n g c) -> p n g c", n=NG, g=GH)[:, :, :, DK]))
                dve.wait_ge(s["okc"], b + 1)
                link(dve.scalar_tensor_tensor(out=qbk[:, b], in0=sumq[:, b], scalar=1.01 * CLIP, in1=nrm[:, b],
                                              op0=ALU.mult, op1=ALU.is_le))
                dve.tensor_reduce(out=count[:, b:b + 1], in_=qbk[:, b], axis=AX.X, op=ALU.min).then_inc(s["cnt"], 1)
                dve.wait_ge(s["cnt"], 2 * b + 2)
                dve.tensor_scalar(flag[0:1, b:b + 1], ps[0:1, 4 * b + 1, 0:1], -1.0, 128.0, ALU.mult, ALU.add).then_inc(s["flag"], 1)

            def clip_path(b):
                with dve.If(bad_rows(dve, b)):
                    dve.memset(facc[:], 0.0).then_inc(f_clr[b], 1)
                    with dve.Fori(0, NG) as n:
                        dve.wait_ge(f_C[b], n + 1)
                        dve.tensor_scalar(fC, ps[:, 4 * b + 3, :], CLIP, None, ALU.mult).then_inc(f_Cc[b], 1)
                        with dve.Fori(0, NK) as c:
                            it = n * NK + c
                            dve.wait_ge(f_Cc[b], n + 1)
                            dve.wait_ge(f_clr[b], n + 1)
                            dve.wait_ge(f_ex[b], it + 1)
                            dve.tensor_tensor(fe, fe, fC, ALU.max).then_inc(f_max[b], 1)
                            dve.wait_ge(f_pv[b], it + 2)
                            for j in range(GH):
                                q = slice(32 * j, 32 * j + DK + 1)
                                last = dve.tensor_tensor(facc[q, :], facc[q, :], ps[q, 4 * b + 2, 0:128], ALU.add)
                            last.then_inc(f_add[b], 1)
                            dve.wait_ge(f_add[b], it + 1)
                        dve.wait_ge(d_fs[b], (n + 1) * 16)
                        dve.memset(facc[:], 0.0).then_inc(f_clr[b], 1)
                    dve.wait_ge(f_end[b], 1)

            def heads_turned(b):
                dve.wait_ge(s["cnT"], b + 1)
                dve.tensor_copy(cnT[:, b * S:(b + 1) * S], ps[:, 4 * b + 1, 0:128]).then_inc(s["cnTc"], 1)

            def project_in(b):
                dve.wait_ge(s["o"], b + 1)
                link(dve.tensor_tensor(xs[:, b, :], xs[:, b, :], ps[:, 4 * b + 1, 128:256], ALU.add))
                variances([b])

            def rotate(b):
                dve.wait_ge(s["qkv"], b + 1)
                qk = ps[:, 4 * b + 2, 0:2 * D].rearrange("p (h a d) -> p h a d", h=2 * H, a=2)
                t, u = (rope[b][:, n].rearrange("p (h a d) -> p h a d", h=2 * H, a=2) for n in range(2))
                cs, sn = (rot[:, n, :].rearrange("p (a d) -> p a d", a=2) for n in range(2))
                h2 = [128, 2 * H, DK // 2]
                for a in range(2):
                    dve.tensor_tensor(t[:, :, a], qk[:, :, a], cs[:, a].unsqueeze(1).broadcast_to(h2), ALU.mult)
                    last = dve.tensor_tensor(u[:, :, a], qk[:, :, 1 - a], sn[:, a].unsqueeze(1).broadcast_to(h2), ALU.mult)
                link(last)
                dve.tensor_tensor(rope[b][:, 2], rope[b][:, 0], rope[b][:, 1], ALU.add).then_inc(s["rope"], 1)

            def qk_turned(b):
                dve.wait_ge(s["qkT"], b + 1)
                dve.tensor_copy(qT[:, b, :], ps[:, 4 * b + 3, 0:128])
                dve.tensor_tensor(kq[:, b], ps[:, 4 * b + 3, 128:256].unsqueeze(1).broadcast_to([128, GH, 128]),
                                  quart[:].unsqueeze(2).broadcast_to([128, GH, 128]), ALU.mult).then_inc(s["qkTc"], 1)

            def self_unit(u):
                b, hs = u // NG, slice(GH * (u % NG), GH * (u % NG) + GH)
                dve.wait_ge(s["s2"], u + 1)
                link(dve.scalar_tensor_tensor(out=sc[b][:, hs, :].rearrange("p h k -> p (h k)"), in0=ps[:, u, :], scalar=SCALE,
                                              in1=alibi[:, hs, :].rearrange("p h k -> p (h k)"), op0=ALU.mult, op1=ALU.add))
                link(dve.tensor_reduce(out=sm[:, b, hs], in_=sc[b][:, hs, :], axis=AX.X, op=ALU.max))
                dve.tensor_scalar(sm[:, b, hs], sm[:, b, hs], -1.0, None, ALU.mult).then_inc(s["sc2"], 1)

            def weights_back(u):
                dve.wait_ge(s["pT"], u + 1)
                dve.tensor_copy(pT[u // NG][:, 4 * (u % NG):4 * (u % NG) + 4, :],
                                ps[:, u, :].rearrange("p (h k) -> p h k", h=4)).then_inc(s["pTd"], 1)

            def heads_turned2(b):
                dve.wait_ge(s["cnT"], B + b + 1)
                dve.tensor_copy(cnT[:, b * S:(b + 1) * S], ps[:, TAIL[b], 0:128]).then_inc(s["cnTc"], 1)

            def project_in2(b):
                dve.wait_ge(s["o"], B + b + 1)
                link(dve.tensor_tensor(xs[:, b, :], xs[:, b, :], ps[:, TAIL[b], 128:256], ALU.add))
                variances([b])

            def sums2(b):
                dve.wait_ge(s["pv2"], b + 1)
                dve.tensor_copy(oS[:, b, :], ps[:, 4 * b, :]).then_inc(s["oS"], 1)

            norms_max()
            norms_over_all()
            bound_terms()
            for n in range(len(UNITS)):
                maxima(n)
                if n == 7:
                    rows(0)
                elif n % 8 == 0 and n > 8:
                    rows(n // 8 - 1)
            lowest(0)
            rows(B * NG - 1)
            check(0)
            clip_path(0)
            normalise(0, 0, 0)
            heads_turned(0)
            dve.wait_ge(s["tab"], 1)
            project_in(0)
            normed(1, [0])
            normed_turned(1, [0], ps[:, 1, 256:384])
            rotate(0)
            qk_turned(0)
            dve.wait_ge(s["pv"], NK * NG * B)
            dve.tensor_copy(oS[:, 1, :], ps[:, 7, :]).then_inc(s["oS"], 1)
            lowest(1)
            self_unit(0)
            check(1)
            self_unit(1)
            clip_path(1)
            normalise(1, 4, 0)
            self_unit(2)
            weights_back(0)
            heads_turned(1)
            self_unit(3)
            project_in(1)
            normed(2, [1])
            normed_turned(2, [1], ps[:, 5, 256:384])
            weights_back(2)
            rotate(1)
            qk_turned(1)
            self_unit(4)
            sums2(0)
            self_unit(5)
            weights_back(4)
            self_unit(6)
            self_unit(7)
            normalise(0, 1, B)
            link(dve.tensor_tensor(xs[:], xs[:], pbB[:].unsqueeze(1).broadcast_to([128, B, D]), ALU.add))
            heads_turned2(0)
            weights_back(6)
            project_in2(0)
            normed(3, [0])
            sums2(1)
            normed_turned(3, [0], ps[:, TAIL[0], 256:384])
            normalise(1, 5, B)
            heads_turned2(1)
            project_in2(1)
            normed(4, [1])
            normed_turned(4, [1], ps[:, TAIL[1], 256:384])

            x2 = qsq[:].rearrange("p (b d) -> p b d", b=B)
            link(dve.tensor_tensor(x2, xn[:], xn[:], ALU.mult))
            link(dve.tensor_reduce(out=x2s[:], in_=x2, axis=AX.X, op=ALU.add))
            dve.wait_ge(s["lgt"], 1)
            link(dve.tensor_tensor(lg[:], ps[:, 6, 0:B * E].rearrange("p (b e) -> p b e", b=B),
                                   x2s[:].unsqueeze(2).broadcast_to([128, B, E]), ALU.subtract))
            link(dve.tensor_reduce(out=lmx[:], in_=lg[:], axis=AX.X, op=ALU.max))
            dve.tensor_tensor(wr[:], lg[:], lmx[:].unsqueeze(2).broadcast_to([128, B, E]), ALU.subtract).then_inc(s["rex"], 1)
            gt, eq = rankw
            for b in range(B):
                f_ = lg[:, b].unsqueeze(1).broadcast_to([128, E, E])
                e_ = lg[:, b].unsqueeze(2).broadcast_to([128, E, E])
                dve.tensor_tensor(gt[:, b], f_, e_, ALU.is_gt)
                last = dve.tensor_tensor(eq[:, b], f_, e_, ALU.is_equal)
            link(last)
            for b in range(B):
                last = dve.tensor_tensor(eq[:, b], eq[:, b], tri[:], ALU.mult)
            link(last)
            link(dve.tensor_tensor(gt.rearrange("p b e f -> p (b e f)"), gt.rearrange("p b e f -> p (b e f)"),
                                   eq.rearrange("p b e f -> p (b e f)"), ALU.add))
            link(dve.tensor_reduce(out=rk[:], in_=gt, axis=AX.X, op=ALU.add))
            dve.wait_ge(s["rex"], 2)
            link(dve.scalar_tensor_tensor(out=wr[:], in0=rk[:], scalar=TOP - 0.5, in1=wr[:], op0=ALU.is_lt, op1=ALU.mult))
            link(dve.tensor_reduce(out=wsum[:], in_=wr[:], axis=AX.X, op=ALU.add))
            link(dve.reciprocal(wsum[:], wsum[:]))
            link(dve.tensor_tensor(wr[:], wr[:], wsum[:].unsqueeze(2).broadcast_to([128, B, E]), ALU.mult))
            link(dve.tensor_copy(wr3[:, :, 0, :], wr[:]))
            link(dve.tensor_tensor(wrr[:], wr[:], wr3[:, :, 0, :], ALU.subtract))
            link(dve.tensor_copy(wr3[:, :, 1, :], wrr[:]))
            dve.tensor_tensor(wr3[:, :, 2, :], wrr[:], wr3[:, :, 1, :], ALU.subtract).then_inc(s["wts"], 1)
            dve.wait_ge(s["wTp"], 1)
            dve.tensor_copy(w3T[:], ps[0:3 * E, 5, 0:B * S // 2].bitcast(bf16)).then_inc(s["wTc"], 1)
            dve.wait_ge(s["wTp"], 2)
            dve.tensor_copy(wT[:], ps[0:E, 7, 0:B * S]).then_inc(s["wTc"], 1)
            for e in range(E):
                dve.wait_ge(s["gelu"], FC * (e + 1))
                dve.wait_ge(s["wb"], e + 1)
                dve.tensor_tensor(hid[e % AHEAD], hid[e % AHEAD],
                                  ps[:, 4 + e % 2, 0:B * S].unsqueeze(1).broadcast_to([128, FC, B * S]), ALU.mult)\
                    .then_inc(s["mul"], 1)
            dve.wait_ge(s["down"], E)
            dve.tensor_copy(yT, ps[:, 6, 0:B * S]).then_inc(s["yc"], 1)
            dve.wait_ge(s["yt"], 1)
            dve.tensor_tensor(xs[:], xs[:], ps[:, 7, 0:B * D].rearrange("p (b d) -> p b d", b=B), ALU.add).then_inc(s["x1"], 1)

        @block.scalar
        def _(act):
            act.wait_ge(s["pool"], 1)
            act.activation(zero[:, 0:B], expo[:, 0:B], ACT.Exp)
            act.wait_ge(d_w, 16 * 2)

            def k_first(u):
                act.wait_ge(s["kproj"], u + 1)
                act.activation(kp[:, u // 2, 0, 512 * (u % 2):512 * (u % 2) + 512], ps[:, u % 4, :], ACT.Identity,
                               bias=cols[:, 1:2]).then_inc(s["k0"], 1)

            def k_square(u):
                act.wait_ge(s["kr"], u // 2 + 1)
                act.activation(ksq[:, u, :], ps[:, u % 4, :], ACT.Square).then_inc(s["ksq"], 1)

            def v_piece(n):
                act.wait_ge(s["v"], n + 1)
                act.activation(vau[:, 4 * n:4 * n + 4, :, 0:DK], ps[:, 4 + n % 2, :].rearrange("p (c h d) -> p c h d", c=4, h=H),
                               ACT.Copy).then_inc(s["va"], 1)

            k_first(0)
            k_first(1)
            k_first(2)
            k_first(3)
            act.wait_ge(s["q"], 1)
            act.activation(qf[:], ps[:, 7, 0:B * S], ACT.Identity, bias=cols[:, 0:1]).then_inc(s["qf"], 1)
            act.activation(qp[:, 0:3, :], ps[:, 7, 0:B * S].unsqueeze(1).broadcast_to([128, 3, B * S]), ACT.Identity,
                           bias=cols[:, 0:1]).then_inc(s["qf"], 1)
            k_square(0)
            k_square(1)
            v_piece(0)
            k_first(4)
            k_first(5)
            k_square(2)
            k_square(3)
            v_piece(1)
            k_first(6)
            k_first(7)
            k_square(4)
            k_square(5)
            v_piece(2)
            k_square(6)
            k_square(7)
            for n in range(3, B * NG):
                v_piece(n)
            def least(b):
                act.wait_ge(s["lowa"], b + 1)
                act.activation(nrm[:, b], low[:, b], ACT.Exp, scale=SCALE).then_inc(s["okc"], 1)

            def clip_path(b):
                with act.If(bad_rows(act, b)):
                    with act.Fori(0, NG * NK) as it:
                        act.wait_ge(f_sc[b], it + 1)
                        act.activation(fe, ps[:, 4 * b + 1, :], ACT.Exp, scale=SCALE).then_inc(f_ex[b], 1)

            def v_self(b):
                act.wait_ge(s["qkv"], b + 1)
                act.wait_ge(s["rope"], b + 1)
                act.activation(vau[:, b, :, 0:DK], ps[:, 4 * b + 2, 2 * D:3 * D].rearrange("p (h d) -> p h d", h=H), ACT.Copy)\
                    .then_inc(s["v2"], 1)

            def self_exp(u):
                act.wait_ge(s["sc2"], u + 1)
                b = u // NG
                for h in range(GH * (u % NG), GH * (u % NG) + GH):
                    last = act.activation(sc[b][:, h, :], sc[b][:, h, :], ACT.Exp, bias=sm[:, b, h:h + 1])
                last.then_inc(s["ex2"], 1)

            def weights_back(u):
                act.wait_ge(s["pT"], u + 1)
                act.activation(pT[u // NG][:, 4 * (u % NG):4 * (u % NG) + 4, :], ps[:, u, :].rearrange("p (h k) -> p h k", h=4),
                               ACT.Copy).then_inc(s["pTa"], 1)

            for g in range(B * NG):
                for c in range(NK):
                    n = NK * g + c
                    act.wait_ge(s["scB"], n + 1)
                    if n >= NE:
                        act.wait_ge(s["pv"], n - NE + 1)
                    act.activation(ex[:, n % NE, :], ps[:, 4 + n % 2, :], ACT.Exp, scale=SCALE).then_inc(s["exp"], 1)
                    if n == NK * NG + LAG:
                        act.wait_ge(s["pv"], NK * NG)
                        act.activation(oS[:, 0, :], ps[:, 6, :], ACT.Copy).then_inc(s["oS"], 1)
                    if n == CHECK:
                        least(0)
                    if n == CHECK + 5:
                        clip_path(0)
            act.wait_ge(d_const, 16 * N_CONST)
            act.activation(sel3b[:], sel3[:], ACT.Copy).then_inc(s["selb"], 1)
            least(1)
            v_self(0)
            self_exp(0)
            clip_path(1)
            self_exp(1)
            weights_back(1)
            self_exp(2)
            self_exp(3)
            weights_back(3)
            v_self(1)
            self_exp(4)
            self_exp(5)
            weights_back(5)
            self_exp(6)
            self_exp(7)
            weights_back(7)
            act.wait_ge(s["rex"], 1)
            act.activation(wr[:], wr[:], ACT.Exp).then_inc(s["rex"], 1)
            for e in range(E):
                if e >= AHEAD:
                    act.wait_ge(s["down"], e - AHEAD + 1)
                for n in range(FC):
                    act.wait_ge(s["up"], 2 * e + n // 2 + 1)
                    act.activation(hid[e % AHEAD][:, n, :], ps[:, (2 * e + n // 2) % 4, 256 * (n % 2):256 * (n % 2) + 256], ACT.Gelu,
                                   bias=b1s[:, FC * e + n:FC * e + n + 1]).then_inc(s["gelu"], 1)

        @block.tensor
        def _(pe):
            cTf = cT[:].rearrange("p b k -> p (b k)")

            def norms(u):
                pe.wait_ge(s["ksq"], u + 1)
                if u == 0:
                    pe.wait_ge(s["blk"], 1)
                for c in range(4):
                    c0 = H * (4 * u + c)
                    last = pe.matmul(ps[:, 6, c0:c0 + H], ksq[:, u, 128 * c:128 * c + 128], blocksb[:], start=True, stop=True)
                if u == B * NG - 1:
                    last.then_inc(s["kn"], 1)

            def norms_turned():
                pe.wait_ge(s["kmx"], 1)
                pe.transpose(ps[0:B * H, 3, 0:128], kmx[:], ident[:]).then_inc(s["kmxT"], 1)

            def bound():
                pe.wait_ge(s["bndq"], 1)
                for b in range(B):
                    c0 = 256 + H * b
                    pe.matmul(ps[:, 7, c0:c0 + H], qsq[:, b * S:(b + 1) * S], blocks[:], start=True, stop=True)
                    c0 += 2 * B * H
                    pe.matmul(ps[:, 7, c0:c0 + H], qf[:, b * S:(b + 1) * S], blbk[:], start=True, stop=True)
                pe.wait_ge(s["bnd"], 1)
                pe.matmul(ps[:, 7, 256 + B * H:256 + 2 * B * H], kbc[:], ident[0:B * H, 0:B * H], start=True, stop=True)\
                    .then_inc(s["bnd"], 1)

            def keys(u):
                if u == 0:
                    pe.wait_ge(d_c0, 16)
                else:
                    pe.wait_ge(d_c[u // 2], 16)
                if u >= 4:
                    pe.wait_ge(s["ksq"], u - 3)
                    pe.wait_ge(s["kr"], u // 2 - 1)
                pe.matmul(ps[:, u % 4, :], wks[:], cTf[:, 512 * u:512 * u + 512], start=True, stop=True)\
                    .then_inc(s["kproj"], 1)

            def vals(n):
                if n >= 2:
                    pe.wait_ge(s["va"], n - 1)
                pe.wait_ge(d_wv, 16)
                for j in range(4):
                    c = 4 * n + j
                    last = pe.matmul(ps[:, 4 + n % 2, 128 * j:128 * j + 128], cTf[:, 128 * c:128 * c + 128], wvs[:],
                                     start=True, stop=True)
                last.then_inc(s["v"], 1)

            pe.wait_ge(d_w, 16 * 2)
            keys(0)
            keys(1)
            pe.wait_ge(s["xn"], 1)
            for b in range(B):
                last = pe.transpose(ps[:, 7, b * S:(b + 1) * S], xn[:, b, :], ident[:])
            last.then_inc(s["xT"], 1)
            keys(2)
            keys(3)
            pe.wait_ge(s["xTc"], 1)
            pe.wait_ge(d_wq, 16)
            pe.matmul(ps[:, 7, 0:B * S], wqs[:], xT[:], start=True, stop=True).then_inc(s["q"], 1)
            vals(0)
            keys(4)
            keys(5)
            vals(1)
            keys(6)
            keys(7)
            vals(2)
            vals(3)

            def unit(n):
                u, b, h, f = UNITS[n]
                if u == 0:
                    pe.wait_ge(d_q, 32)
                    pe.wait_ge(s["ksq"], NG * B)
                    pe.wait_ge(s["kr"], 2 * B)
                for i, (bs, p0, _) in enumerate(STACKS):
                    if (bs, p0, 0, 0) == (b, h // 2, h % 2, f):
                        pe.wait_ge(d_kb[i], 32 * len(K_RUNS))
                if u >= 2:
                    pe.wait_ge(s["redA"], u - 1)
                for j in range(2):
                    k0 = 1024 * f + 512 * j
                    last = pe.matmul(ps[:, 2 * (u % 2) + j, :], qst[:, h // 2, h % 2, b * S:(b + 1) * S],
                                     kst[:, b, h // 2, k0:k0 + 512], start=True, stop=True)
                last.then_inc(s["unitA"], 1)

            def turn(g):
                pe.wait_ge(s["mpad"], g + 1)
                if g:
                    pe.wait_ge(s["mrow"], g)
                else:
                    pe.wait_ge(s["zb"], 2)
                if g == NG + 1:
                    pe.wait_ge(s["oS"], 1)
                for r in range(2):
                    last = pe.transpose(ps[:, turn_bank(g), 64 * r:64 * r + 64].bitcast(bf16), mpad[:, g % 2, r, :], identb[:])
                last.then_inc(s["mT"], 1)

            def scores(g, c):
                b, r = g // NG, 2 * (g % NG)
                n = NK * g + c
                if c == 0:
                    pe.wait_ge(s["mrow"], g + 1)
                if n == 0:
                    pe.wait_ge(s["va"], B * NK // 4)
                if n >= 2:
                    pe.wait_ge(s["exp"], n - 1)
                for j in range(2):
                    last = pe.matmul(ps[:, 4 + n % 2, 256 * j:256 * j + 256], kst[:, b, r + j, 128 * c:128 * c + 128],
                                     qst[:, r + j, :, b * S:(b + 1) * S], start=True, stop=True)
                last.then_inc(s["scB"], 1)

            def values(g, c):
                b, hg = g // NG, g % NG
                n = NK * g + c
                pe.wait_ge(s["exp"], n + 1)
                if g % NG == 0 and c % 4 == 0:
                    pe.wait_ge(s["vau"], NG * b + c // 4 + 1)
                if n == NK * NG:
                    pe.wait_ge(s["mrow"], NG + 1)
                for j in range(GH):
                    last = pe.matmul(ps[32 * j:32 * j + DK + 1, 6 + b, 128 * hg:128 * hg + 128],
                                     vau[:, NK * b + c, GH * hg + j, :], ex[:, n % NE, 128 * j:128 * j + 128],
                                     start=(c == 0), stop=(c == NK - 1), tile_position=(0, 32 * j))
                last.then_inc(s["pv"], 1)

            nu = 0

            def ahead(n):
                if n < len(UNITS):
                    unit(n)
                if n == 7:
                    vals(6)
                    vals(7)
                    turn(0)

            for u in range(B * NG):
                norms(u)
            vals(4)
            norms_turned()
            vals(5)
            bound()
            for nu in range(8 + LEAD):
                ahead(nu)
            nu = 8 + LEAD
            def turn_sums(b):
                for n in range(NG):
                    last = pe.transpose(ps[:, 4 * b, 128 * n:128 * n + 128], oS[:, b, 128 * n:128 * n + 128], ident[:])
                return last

            def sums_out(b):
                pe.wait_ge(s["oS"], b + 1)
                if b == 0:
                    pe.wait_ge(s["redA"], len(UNITS))
                else:
                    pe.wait_ge(s["exp"], B * NG * NK)
                turn_sums(b).then_inc(s["oT"], 1)

            def count_good(b):
                pe.wait_ge(s["cnt"], 2 * b + 1)
                pe.matmul(ps[0:1, 4 * b + 1, 0:1], count[:, b:b + 1], onec[:, 0:1], start=True, stop=True).then_inc(s["cnt"], 1)

            def clip_path(b):
                with pe.If(bad_rows(pe, b)):
                    pe.wait_ge(d_const, 16 * N_CONST)
                    pe.sem_inc(f_pv[b], 1)
                    with pe.Fori(0, NG) as n:
                        pe.wait_ge(d_fg[b], (n + 1) * 48)
                        for j in range(GH):
                            last = pe.matmul(ps[:, 4 * b + 3, 128 * j:128 * j + 128], sumrow[:, j:j + 1].broadcast_to([128, 128]),
                                             fo[:], start=True, stop=True)
                        last.then_inc(f_C[b], 1)
                        with pe.Fori(0, NK) as c:
                            it = n * NK + c
                            pe.wait_ge(d_fc[b], (it + 1) * 32)
                            for j in range(2):
                                last = pe.matmul(ps[:, 4 * b + 1, 256 * j:256 * j + 256], fk[:, j, :],
                                                 fq[:, j].rearrange("p a n -> p (a n)"), start=True, stop=True)
                            last.then_inc(f_sc[b], 1)
                            pe.wait_ge(f_max[b], it + 1)
                            for j in range(GH):
                                last = pe.matmul(ps[32 * j:32 * j + DK + 1, 4 * b + 2, 0:128], fv[:, j, :], fe[:, 128 * j:128 * j + 128],
                                                 start=True, stop=True, tile_position=(0, 32 * j))
                            last.then_inc(f_pv[b], 1)
                            pe.wait_ge(f_add[b], it + 1)
                    pe.wait_ge(d_fs[b], NG * 16)
                    turn_sums(b).then_inc(f_end[b], 1)

            def turn_heads(b):
                pe.wait_ge(s["cn"], b + 1)
                pe.transpose(ps[:, 4 * b + 1, 0:128], cn[:, b, :], ident[:]).then_inc(s["cnT"], 1)

            def project_out(b):
                pe.wait_ge(s["cnTc"], b + 1)
                pe.wait_ge(d_const, 16 * N_CONST)
                pe.matmul(ps[:, 4 * b + 1, 128:256], cnT[:, b * S:(b + 1) * S], wos[:], start=True, stop=True).then_inc(s["o"], 1)

            def turn_normed(b):
                pe.wait_ge(s["xn"], b + 2)
                pe.transpose(ps[:, 4 * b + 1, 256:384], xn[:, b, :], ident[:]).then_inc(s["xT"], 1)

            def project_qkv(b):
                pe.wait_ge(s["xTc"], b + 2)
                pe.matmul(ps[:, 4 * b + 2, 0:3 * D], xT[:, b * S:(b + 1) * S], qkvs[:], start=True, stop=True).then_inc(s["qkv"], 1)

            def turn_qk(b):
                pe.wait_ge(s["rope"], b + 1)
                for a in range(2):
                    last = pe.transpose(ps[:, 4 * b + 3, 128 * a:128 * a + 128], rope[b][:, 2, 128 * a:128 * a + 128], ident[:])
                last.then_inc(s["qkT"], 1)

            def first_batch(n):
                if n == CHECK + 2:
                    sums_out(0)
                if n == CHECK + 4:
                    count_good(0)
                if n == CHECK + 5:
                    clip_path(0)
                if n == CHECK + 7:
                    turn_heads(0)
                if n == CHECK + 9:
                    project_out(0)
                if n == CHECK + 12:
                    turn_normed(0)
                if n == CHECK + 14:
                    project_qkv(0)
                if n == CHECK + 17:
                    turn_qk(0)

            for g in range(B * NG):
                for c in range(NK):
                    scores(g, c)
                    if c == NK - 2 and g + 1 < B * NG:
                        turn(g + 1)
                    if c % 2 == 0 and nu < len(UNITS):
                        ahead(nu)
                        nu += 1
                    if NK * g + c >= LAG:
                        values(*divmod(NK * g + c - LAG, NK))
                    first_batch(NK * g + c)
            for n in range(B * NG * NK - LAG, B * NG * NK):
                values(*divmod(n, NK))

            def scores2(u):
                b, n = u // NG, u % NG
                r = slice(32 * n, 32 * n + 32)
                if n == 0:
                    pe.wait_ge(s["qkTc"], b + 1)
                if n == 2:
                    pe.wait_ge(s["v2"], b + 1)
                pe.matmul(ps[:, u, :], qT[r, b, :], kq[r, b].rearrange("p h k -> p (h k)"),
                          start=True, stop=True, tile_position=(32 * n, 0)).then_inc(s["s2"], 1)

            def turn_weights(u):
                pe.wait_ge(s["ex2"], u + 1)
                for j in range(GH):
                    last = pe.transpose(ps[:, u, 128 * j:128 * j + 128], sc[u // NG][:, GH * (u % NG) + j, :], ident[:])
                last.then_inc(s["pT"], 1)

            def attend(u):
                b, n = u // NG, u % NG
                if u % 2:
                    pe.wait_ge(s["pTa"], u // 2 + 1)
                else:
                    pe.wait_ge(s["pTd"], u // 2 + 1)
                for j in range(GH):
                    last = pe.matmul(ps[32 * j:32 * j + DK + 1, 4 * b, 128 * n:128 * n + 128], vau[:, b, GH * n + j, :],
                                     pT[b][:, GH * n + j, :], start=True, stop=True, tile_position=(0, 32 * j))
                if n == NG - 1:
                    last.then_inc(s["pv2"], 1)

            def turn_heads2(b):
                pe.wait_ge(s["cn"], B + b + 1)
                pe.transpose(ps[:, TAIL[b], 0:128], cn[:, b, :], ident[:]).then_inc(s["cnT"], 1)

            def project_out2(b):
                pe.wait_ge(s["cnTc"], B + b + 1)
                pe.matmul(ps[:, TAIL[b], 128:256], cnT[:, b * S:(b + 1) * S], projs[:], start=True, stop=True).then_inc(s["o"], 1)

            def turn_normed2(b):
                pe.wait_ge(s["xn"], B + b + 2)
                pe.transpose(ps[:, TAIL[b], 256:384], xn[:, b, :], ident[:]).then_inc(s["xT"], 1)

            def up_part(e, b, n0):
                for n in (n0, n0 + 1):
                    f0, c0 = F * e + 128 * n, 256 * (n % 2) + S * b
                    last = pe.matmul(ps[:, (2 * e + n // 2) % 4, c0:c0 + S], w1s[:, f0:f0 + 128], xT[:, b * S:(b + 1) * S],
                                     start=True, stop=True)
                if b == B - 1:
                    last.then_inc(s["up"], 1)

            def turn_sums2(b):
                pe.wait_ge(s["oS"], B + b + 1)
                for n in range(NG):
                    last = pe.transpose(ps[:, 4 * b + 1, 128 * n:128 * n + 128], oS[:, b, 128 * n:128 * n + 128], ident[:])
                last.then_inc(s["oT"], 1)

            scores2(0)
            sums_out(1)
            scores2(1)
            count_good(1)
            scores2(2)
            clip_path(1)
            turn_weights(0)
            turn_heads(1)
            scores2(3)
            project_out(1)
            turn_weights(1)
            attend(0)
            turn_normed(1)
            turn_weights(2)
            attend(1)
            project_qkv(1)
            turn_weights(3)
            attend(2)
            turn_qk(1)
            attend(3)
            for u in range(4, 7):
                scores2(u)
            turn_weights(4)
            scores2(7)
            turn_weights(5)
            attend(4)
            turn_sums2(0)
            turn_weights(6)
            attend(5)
            turn_heads2(0)
            turn_weights(7)
            project_out2(0)
            attend(6)
            attend(7)
            turn_normed2(0)
            turn_sums2(1)
            pe.wait_ge(d_wt, 16 * 4)
            pe.wait_ge(s["xTc"], 4)
            up_part(0, 0, 0)
            turn_heads2(1)
            up_part(0, 0, 2)
            project_out2(1)

            pe.wait_ge(s["tab"], 1)
            logits = [ps[:, 6, E * b:E * (b + 1)] for b in range(B)]
            pe.matmul(ps[:, 6, 0:B * E], neg[:], ksq2[:].unsqueeze(1).broadcast_to([128, B, E]), start=True, stop=False)
            pe.matmul(ps[:, 6, 0:B * E], onec[0:1, :], rb_s[:].unsqueeze(1).broadcast_to([1, B, E]), start=False, stop=False)
            up_part(1, 0, 0)
            up_part(1, 0, 2)
            turn_normed2(1)
            for b in range(B):
                pe.wait_ge(s["xTc"], 4 + b)
                last = pe.matmul(logits[b], xT[:, b * S:(b + 1) * S], gk[:], start=False, stop=(b == B - 1))
            last.then_inc(s["lgt"], 1)

            def up(e):
                if e >= 2:
                    pe.wait_ge(s["gelu"], FC * (e - 1))
                for n in range(FC):
                    f0 = F * e + 128 * n
                    last = pe.matmul(ps[:, (2 * e + n // 2) % 4, 256 * (n % 2):256 * (n % 2) + 256], w1s[:, f0:f0 + 128], xT[:],
                                     start=True, stop=True)
                    if n % 2:
                        last.then_inc(s["up"], 1)

            def weights(e):
                if e >= 2:
                    pe.wait_ge(s["mul"], e - 1)
                if e == 1:
                    pe.wait_ge(s["wTc"], 2)
                pe.matmul(ps[:, 4 + e % 2, 0:B * S], sel3b[:, e:e + 1].broadcast_to([3 * E, 128]), w3T[:], start=True, stop=True)\
                    .then_inc(s["wb"], 1)

            def down(e):
                pe.wait_ge(s["mul"], e + 1)
                for n in range(FC):
                    last = pe.matmul(ps[:, 6, 0:B * S], w2s[:, FC * e + n, :], hid[e % AHEAD][:, n, :],
                                     start=False, stop=(e == E - 1 and n == FC - 1))
                last.then_inc(s["down"], 1)

            for e in range(2):
                up_part(e, 1, 0)
                up_part(e, 1, 2)
            up(2)
            pe.wait_ge(s["wts"], 1)
            for b in range(B):
                last = pe.transpose(ps[0:3 * E, 5, b * S // 2:(b + 1) * S // 2].bitcast(bf16),
                                    wr3[:, b].rearrange("p t e -> p (t e)"), identb[:])
            last.then_inc(s["wTp"], 1)
            for b in range(B):
                last = pe.transpose(ps[0:E, 7, b * S:(b + 1) * S], wr[:, b, :], ident[:])
            last.then_inc(s["wTp"], 1)
            pe.wait_ge(s["selb"], 1)
            pe.wait_ge(s["wTc"], 1)
            weights(0)
            up(3)
            pe.wait_ge(s["wTc"], 2)
            pe.matmul(ps[:, 6, 0:B * S], b2s[:], wT[:], start=True, stop=False)
            pe.wait_ge(d_w2, 16 * 4)
            for e in range(E):
                if e + 1 < E:
                    weights(e + 1)
                down(e)
                if e + AHEAD < E:
                    up(e + AHEAD)
            pe.wait_ge(s["yc"], 1)
            for b in range(B):
                last = pe.transpose(ps[:, 7, D * b:D * b + D], yT[:, b * S:(b + 1) * S], ident[:])
            last.then_inc(s["yt"], 1)


ROWS = np.arange(D).reshape(PAIRS, 2, DK).transpose(1, 2, 0).reshape(D)


def shape_tables():
    ident = np.eye(128, dtype=np.float32)
    blocks = np.eye(H, dtype=np.float32)[ROWS // DK]
    inv = (np.float32(1.0) / np.float32(10000.0) ** (np.arange(0, DK, 2, dtype=np.float32) / np.float32(DK)))
    freqs = np.arange(S, dtype=np.float32)[:, None] * inv[None, :].astype(np.float32)
    sin, cos = np.sin(freqs), np.cos(freqs)
    rot = np.stack([np.concatenate([cos, cos], 1), np.concatenate([-sin, sin], 1)], 1).astype(np.float32)
    pos = np.arange(S, dtype=np.float32)
    dist = np.minimum(pos[None, :] - pos[:, None], 0).astype(np.float32)
    tri = np.broadcast_to(np.tril(np.ones((E, E), np.float32), -1)[None], (128, E, E)).copy()
    quart = np.tile(np.repeat(np.eye(GH, dtype=np.float32), DK, axis=0), (NG, 1))
    sumrow = np.zeros((128, GH), np.float32)
    sumrow[32 * np.arange(GH) + DK, np.arange(GH)] = 1
    return {"ident": ident, "blocks": blocks, "rot": rot, "dist": dist, "tri": tri, "quart": quart, "sumrow": sumrow, "sel3": np.tile(np.eye(E, dtype=np.float32), (3, 1)),}


def kernel(**inputs):
    import numpy as _np
    import concourse.bacc as _bacc
    from concourse import mybir as _mybir
    from concourse.bass_utils import run_bass_kernel_spmd as _run

    i = {k: _np.asarray(v) for k, v in inputs.items()}
    p = "L0_xattn_"
    arrays = {
        "x": i["x"],
        "ctxT": i["ctx_1024"].transpose(0, 2, 1),
        "wq": i[p + "Wq"][ROWS].T, "wk": i[p + "Wk"][ROWS].T, "wv": i[p + "Wv"].T, "wo": i[p + "Wo"].T,
        "bqk": _np.stack([i[p + "bq"][ROWS], i[p + "bk"][ROWS]], axis=1), "bv": i[p + "bv"][None], "bo": i[p + "bo"][None],
        "qkvw": i["L0_attn_qkv_w"].T, "projw": i["L0_attn_proj_w"].T, "projb": i["L0_attn_proj_b"][None],
        "slopes": i["L0_attn_slopes"][None],
        "keysT": i["L0_ffn_keys"].T,
        "w1": i["L0_ffn_w1"].transpose(2, 0, 1).reshape(D, E * F),
        "b1": i["L0_ffn_b1"].reshape(E * FC, 128).T,
        "w2": i["L0_ffn_w2"].reshape(E, D, FC, 128).transpose(3, 0, 2, 1).reshape(128, E * FC, D),
        "b2": i["L0_ffn_b2"], "rwT": i["L0_ffn_rw"].T, "rb": i["L0_ffn_rb"][None],
        **shape_tables(),
    }
    nc = _bacc.Bacc("TRN2", target_bir_lowering=False, num_devices=1)
    feed, args = {}, []
    for name, a in arrays.items():
        feed["in_" + name] = _np.ascontiguousarray(a)
        args.append(nc.dram_tensor("in_" + name, a.shape, _mybir.dt.from_np(a.dtype), kind="ExternalInput").ap())
    args.append(nc.dram_tensor("out_x", (B, S, D), _mybir.dt.float32, kind="ExternalOutput").ap())
    build(nc, *args)
    return _run(nc, [feed], core_ids=[0]).results[0]["out_x"]
```
